# Optimizing a Trainium2 kernel written in Bass

```python
import numpy as np
import jax
import jax.numpy as jnp

def _softmax(x, axis=-1):
    return jax.nn.softmax(x, axis=axis)

def _gelu(x):
    return jax.nn.gelu(x, approximate=True)

def _silu(x):
    return jax.nn.silu(x)

def _sigmoid(x):
    return jax.nn.sigmoid(x)

def _layernorm(x, axis=-1, eps=1e-05):
    m = jnp.mean(x, axis=axis, keepdims=True)
    v = jnp.var(x, axis=axis, keepdims=True)
    return (x - m) / jnp.sqrt(v + eps)

def _scatter_add(tgt, idx, src, axis=0):
    return tgt.at[idx].add(src)

def _segment_sum(src, seg, n):
    return jax.ops.segment_sum(src, seg, n)
kernel_name = 'mk_decoder_postln_d2_seqx_r8_8460fa'

def setup_inputs(seed: int=0):
    np.random.seed(seed)
    _w = jnp.asarray

    def _rec_inputs():
        import jax
        import jax.numpy as jnp
        _rk = jax.random.key(seed)
        x = 6.313e-05 + 0.9998 * jax.random.normal(jax.random.fold_in(_rk, 1), (16, 128, 128), jnp.float32)
        _lenS = 128 - jax.random.randint(jax.random.fold_in(_rk, 7), (16,), 0, max(1, 128 // 4) + 1, jnp.int32)
        _lenS2 = 128 - jax.random.randint(jax.random.fold_in(_rk, 8), (16,), 0, max(1, 128 // 4) + 1, jnp.int32)
        _ctx_1024P = jax.random.normal(jax.random.fold_in(_rk, 11), (16, 16, 128), jnp.float32)
        _ctx_1024c = jax.random.dirichlet(jax.random.fold_in(_rk, 511), 0.3 * jnp.ones((16,), jnp.float32), (16, 128))
        _ctx_1024t = jnp.einsum('bsk,bkd->bsd', _ctx_1024c, _ctx_1024P)
        _ctx_1024t = _ctx_1024t * jax.lax.rsqrt(jnp.mean(jnp.square(_ctx_1024t)) + 1e-12) * 0.953939
        ctx_1024 = -0.000214406 + 1.00034 * (_ctx_1024t + 0.3 * jax.random.normal(jax.random.fold_in(_rk, 611), (16, 128, 128), jnp.float32))
        return (x, ctx_1024)
    x, ctx_1024 = _rec_inputs()

    def _L0_attn_setup():
        import jax, jax.numpy as jnp
        import numpy as np
        DIM = 128
        HEADS = 16
        DIM_HEAD = 64
        INNER = HEADS * DIM_HEAD

        def _attention(x, ln_gamma, ln_beta, w_qkv, w_out, b_out):
            b, n, _ = x.shape
            scale = DIM_HEAD ** (-0.5)
            mu = jnp.mean(x, axis=-1, keepdims=True)
            var = jnp.var(x, axis=-1, keepdims=True)
            xn = (x - mu) / jnp.sqrt(var + 1e-05) * ln_gamma + ln_beta
            qkv = jnp.einsum('bnd,ed->bne', xn, w_qkv)
            q, k, v = jnp.split(qkv, 3, axis=-1)
            reshape = lambda t: t.reshape(b, n, HEADS, DIM_HEAD).transpose(0, 2, 1, 3)
            q, k, v = (reshape(q) * scale, reshape(k), reshape(v))
            sim = jnp.einsum('bhid,bhjd->bhij', q, k)
            mask_value = -jnp.finfo(sim.dtype).max
            causal = jnp.triu(jnp.ones((n, n), dtype=bool), k=1)
            sim = jnp.where(causal, mask_value, sim)
            sim = sim - jax.lax.stop_gradient(jnp.max(sim, axis=-1, keepdims=True))
            attn = jax.nn.softmax(sim, axis=-1)
            out = jnp.einsum('bhij,bhjd->bhid', attn, v)
            out = out.transpose(0, 2, 1, 3).reshape(b, n, INNER)
            return jnp.einsum('bne,de->bnd', out, w_out) + b_out
        key = jax.random.key(seed)
        ks = jax.random.split(key, 6)
        x = jax.random.normal(ks[0], (2, 256, DIM), dtype=jnp.float32)
        ln_gamma = jnp.ones((DIM,), dtype=jnp.float32)
        ln_beta = jnp.zeros((DIM,), dtype=jnp.float32)
        w_qkv = jax.random.normal(ks[1], (3 * INNER, DIM), dtype=jnp.float32) * DIM ** (-0.5)
        w_out = jax.random.normal(ks[2], (DIM, INNER), dtype=jnp.float32) * INNER ** (-0.5)
        b_out = jax.random.normal(ks[3], (DIM,), dtype=jnp.float32) * 0.02
        return {'x': x, 'ln_gamma': ln_gamma, 'ln_beta': ln_beta, 'w_qkv': w_qkv, 'w_out': w_out, 'b_out': b_out}
    _L0_attn_all = _L0_attn_setup()
    _L0_attn_in = {k: v for k, v in _L0_attn_all.items() if k in ('ln_gamma', 'ln_beta', 'w_qkv', 'w_out', 'b_out')}
    del _L0_attn_all

    def _L0_xattn_setup():
        import jax, jax.numpy as jnp
        import numpy as np
        from jax import lax
        BIG = jnp.float32(1e+30)

        def _pairwise_euclidean(a, b):
            aa = jnp.sum(a * a, axis=-1)[:, None]
            bb = jnp.sum(b * b, axis=-1)[None, :]
            ab = a @ b.T
            return jnp.sqrt(jnp.maximum(aa + bb - 2.0 * ab, 0.0))

        def _dtw_cost(D):
            row0 = jnp.cumsum(D[0])

            def row_step(prev_row, d_row):
                first = d_row[0] + prev_row[0]

                def col_step(left, inp):
                    d_ij, up, diag = inp
                    r = d_ij + jnp.minimum(jnp.minimum(up, left), diag)
                    return (r, r)
                _, rest = lax.scan(col_step, first, (d_row[1:], prev_row[1:], prev_row[:-1]))
                row = jnp.concatenate([first[None], rest])
                return (row, row)
            _, rows = lax.scan(row_step, row0, D[1:])
            return jnp.concatenate([row0[None], rows], axis=0)

        def _backtrack(R, T1, T2):
            L = T1 + T2 - 1

            def step(carry, _):
                i, j, done = carry
                valid = jnp.logical_not(done)
                cd = jnp.where((i > 0) & (j > 0), R[jnp.maximum(i - 1, 0), jnp.maximum(j - 1, 0)], BIG)
                cu = jnp.where(i > 0, R[jnp.maximum(i - 1, 0), j], BIG)
                cl = jnp.where(j > 0, R[i, jnp.maximum(j - 1, 0)], BIG)
                choice = jnp.argmin(jnp.stack([cd, cu, cl]))
                ni = jnp.where(choice <= 1, i - 1, i)
                nj = jnp.where((choice == 0) | (choice == 2), j - 1, j)
                at_origin = (i == 0) & (j == 0)
                ni = jnp.where(at_origin, 0, ni)
                nj = jnp.where(at_origin, 0, nj)
                return ((ni, nj, done | at_origin), (i, j, valid))
            init = (jnp.int32(T1 - 1), jnp.int32(T2 - 1), jnp.bool_(False))
            _, (i_idx, j_idx, valid) = lax.scan(step, init, None, length=L)
            return (i_idx, j_idx, valid)

        def _align_one(small, large):
            T_small, d = small.shape
            T_large = large.shape[0]
            D = _pairwise_euclidean(small, large)
            R = _dtw_cost(D)
            i_idx, j_idx, valid = _backtrack(R, T_small, T_large)
            contrib = small[i_idx] * valid[:, None].astype(small.dtype)
            expanded = jnp.zeros((T_large, d), dtype=small.dtype).at[j_idx].add(contrib)
            return expanded
        key = jax.random.key(seed)
        k1, k2 = jax.random.split(key)
        teacher = jax.random.normal(k1, (16, 50, 128), dtype=jnp.float32)
        student = jax.random.normal(k2, (16, 75, 128), dtype=jnp.float32)
        return {'teacher_features': teacher, 'student_features': student}
    _L0_xattn_all = _L0_xattn_setup()
    _L0_xattn_in = {k: v for k, v in _L0_xattn_all.items() if k in ()}
    del _L0_xattn_all

    def _L0_ffn_setup():
        import jax, jax.numpy as jnp
        import numpy as np
        N_EMBD = 128
        N_EXP = 8
        TOP_K = 2
        CAPACITY = 512
        D_FF = 3 * N_EMBD
        key = jax.random.key(seed)
        k1, k2, k3, k4 = jax.random.split(key, 4)
        x = jax.random.normal(k1, (8, 256, N_EMBD), dtype=jnp.float32)
        w_gate = jax.random.normal(k2, (N_EMBD, N_EXP), dtype=jnp.float32) * 0.02
        c_fc = jax.random.normal(k3, (N_EXP, N_EMBD, D_FF), dtype=jnp.float32) * 0.02
        c_proj = jax.random.normal(k4, (N_EXP, D_FF // 2, N_EMBD), dtype=jnp.float32) * 0.02
        return {'x': x, 'w_gate': w_gate, 'c_fc': c_fc, 'c_proj': c_proj}
    _L0_ffn_all = _L0_ffn_setup()
    _L0_ffn_in = {k: v for k, v in _L0_ffn_all.items() if k in ('w_gate', 'c_fc', 'c_proj')}
    del _L0_ffn_all

    def _L1_attn_setup():
        import jax, jax.numpy as jnp
        import numpy as np
        HEADS = 32
        DIM_HEAD = 32
        EPS = 1e-06
        key = jax.random.key(seed)
        k1, k2, k3 = jax.random.split(key, 3)
        b, n, dim = (2, 256, 128)
        x = jax.random.normal(k1, (b, n, dim), dtype=jnp.float32)
        w_qkv = jax.random.normal(k2, (dim, 3 * HEADS * DIM_HEAD), dtype=jnp.float32) * dim ** (-0.5)
        w_out = jax.random.normal(k3, (HEADS * DIM_HEAD, dim), dtype=jnp.float32) * dim ** (-0.5)
        b_out = jnp.zeros((dim,), dtype=jnp.float32)
        ln_gamma = jnp.ones((dim,), dtype=jnp.float32)
        ln_beta = jnp.zeros((dim,), dtype=jnp.float32)
        return {'x': x, 'w_qkv': w_qkv, 'w_out': w_out, 'b_out': b_out, 'ln_gamma': ln_gamma, 'ln_beta': ln_beta}
    _L1_attn_all = _L1_attn_setup()
    _L1_attn_in = {k: v for k, v in _L1_attn_all.items() if k in ('w_qkv', 'w_out', 'b_out', 'ln_gamma', 'ln_beta')}
    del _L1_attn_all

    def _L1_xattn_setup():
        import jax, jax.numpy as jnp
        import numpy as np
        import math
        D_MODEL = 128
        NHEAD = 16
        HEAD_DIM = D_MODEL // NHEAD
        ROPE_BASE = 10000.0

        def _rope_cos_sin(seq_len, dtype):
            inv_freq = 1.0 / ROPE_BASE ** (jnp.arange(0, HEAD_DIM, 2, dtype=jnp.float32) / HEAD_DIM)
            t = jnp.arange(seq_len, dtype=jnp.float32)
            freqs = jnp.einsum('i,j->ij', t, inv_freq)
            emb = jnp.concatenate([freqs, freqs], axis=-1)
            return (jnp.cos(emb).astype(dtype), jnp.sin(emb).astype(dtype))

        def _rotate_half(x):
            x1, x2 = jnp.split(x, 2, axis=-1)
            return jnp.concatenate([-x2, x1], axis=-1)
        key = jax.random.key(seed)
        ks = jax.random.split(key, 11)
        B, S = (4, 256)
        s = 1.0 / math.sqrt(D_MODEL)
        return {'query': jax.random.normal(ks[0], (B, S, D_MODEL), jnp.float32), 'key': jax.random.normal(ks[1], (B, S, D_MODEL), jnp.float32), 'value': jax.random.normal(ks[2], (B, S, D_MODEL), jnp.float32), 'Wq': jax.random.normal(ks[3], (D_MODEL, D_MODEL), jnp.float32) * s, 'bq': jnp.zeros((D_MODEL,), jnp.float32), 'Wk': jax.random.normal(ks[4], (D_MODEL, D_MODEL), jnp.float32) * s, 'bk': jnp.zeros((D_MODEL,), jnp.float32), 'Wv': jax.random.normal(ks[5], (D_MODEL, D_MODEL), jnp.float32) * s, 'bv': jnp.zeros((D_MODEL,), jnp.float32), 'Wo': jax.random.normal(ks[6], (D_MODEL, D_MODEL), jnp.float32) * s, 'bo': jnp.zeros((D_MODEL,), jnp.float32)}
    _L1_xattn_all = _L1_xattn_setup()
    _L1_xattn_in = {k: v for k, v in _L1_xattn_all.items() if k in ('Wq', 'bq', 'Wk', 'bk', 'Wv', 'bv', 'Wo', 'bo')}
    del _L1_xattn_all

    def _L1_ffn_setup():
        import jax, jax.numpy as jnp
        import numpy as np
        from jax import lax
        T, B, I, M, O = (32, 64, 128, 128, 128)

        def _xavier(key, shape):
            fan_out, fan_in = shape
            limit = float(np.sqrt(6.0 / (fan_in + fan_out)))
            return jax.random.uniform(key, shape, jnp.float32, -limit, limit)
        key = jax.random.key(seed)
        ks = jax.random.split(key, 9)
        x = jax.random.normal(ks[0], (T, B, I), jnp.float32)
        return {'x': x, 'wf': _xavier(ks[1], (M, I)), 'uf': _xavier(ks[2], (M, M)), 'bf': jnp.zeros((M,), jnp.float32), 'wi': _xavier(ks[3], (M, I)), 'ui': _xavier(ks[4], (M, M)), 'bi': jnp.zeros((M,), jnp.float32), 'wc': _xavier(ks[5], (M, I)), 'uc': _xavier(ks[6], (M, M)), 'bc': jnp.zeros((M,), jnp.float32), 'wo': _xavier(ks[7], (O, I)), 'uo': _xavier(ks[8], (O, M)), 'bo': jnp.zeros((O,), jnp.float32), 'in_c': jnp.zeros((M,), jnp.float32)}
    _L1_ffn_all = _L1_ffn_setup()
    _L1_ffn_in = {k: v for k, v in _L1_ffn_all.items() if k in ('wf', 'uf', 'bf', 'wi', 'ui', 'bi', 'wc', 'uc', 'bc', 'wo', 'uo', 'bo', 'in_c')}
    del _L1_ffn_all
    return {'x': x, 'ctx_1024': ctx_1024, 'L0_attn_ln_gamma': _L0_attn_in['ln_gamma'], 'L0_attn_ln_beta': _L0_attn_in['ln_beta'], 'L0_attn_w_qkv': _L0_attn_in['w_qkv'], 'L0_attn_w_out': _L0_attn_in['w_out'], 'L0_attn_b_out': _L0_attn_in['b_out'], 'L0_ffn_w_gate': _L0_ffn_in['w_gate'], 'L0_ffn_c_fc': _L0_ffn_in['c_fc'], 'L0_ffn_c_proj': _L0_ffn_in['c_proj'], 'L1_attn_w_qkv': _L1_attn_in['w_qkv'], 'L1_attn_w_out': _L1_attn_in['w_out'], 'L1_attn_b_out': _L1_attn_in['b_out'], 'L1_attn_ln_gamma': _L1_attn_in['ln_gamma'], 'L1_attn_ln_beta': _L1_attn_in['ln_beta'], 'L1_xattn_Wq': _L1_xattn_in['Wq'], 'L1_xattn_bq': _L1_xattn_in['bq'], 'L1_xattn_Wk': _L1_xattn_in['Wk'], 'L1_xattn_bk': _L1_xattn_in['bk'], 'L1_xattn_Wv': _L1_xattn_in['Wv'], 'L1_xattn_bv': _L1_xattn_in['bv'], 'L1_xattn_Wo': _L1_xattn_in['Wo'], 'L1_xattn_bo': _L1_xattn_in['bo'], 'L1_ffn_wf': _L1_ffn_in['wf'], 'L1_ffn_uf': _L1_ffn_in['uf'], 'L1_ffn_bf': _L1_ffn_in['bf'], 'L1_ffn_wi': _L1_ffn_in['wi'], 'L1_ffn_ui': _L1_ffn_in['ui'], 'L1_ffn_bi': _L1_ffn_in['bi'], 'L1_ffn_wc': _L1_ffn_in['wc'], 'L1_ffn_uc': _L1_ffn_in['uc'], 'L1_ffn_bc': _L1_ffn_in['bc'], 'L1_ffn_wo': _L1_ffn_in['wo'], 'L1_ffn_uo': _L1_ffn_in['uo'], 'L1_ffn_bo': _L1_ffn_in['bo'], 'L1_ffn_in_c': _L1_ffn_in['in_c']}

def reference(x, ctx_1024, L0_attn_ln_gamma, L0_attn_ln_beta, L0_attn_w_qkv, L0_attn_w_out, L0_attn_b_out, L0_ffn_w_gate, L0_ffn_c_fc, L0_ffn_c_proj, L1_attn_w_qkv, L1_attn_w_out, L1_attn_b_out, L1_attn_ln_gamma, L1_attn_ln_beta, L1_xattn_Wq, L1_xattn_bq, L1_xattn_Wk, L1_xattn_bk, L1_xattn_Wv, L1_xattn_bv, L1_xattn_Wo, L1_xattn_bo, L1_ffn_wf, L1_ffn_uf, L1_ffn_bf, L1_ffn_wi, L1_ffn_ui, L1_ffn_bi, L1_ffn_wc, L1_ffn_uc, L1_ffn_bc, L1_ffn_wo, L1_ffn_uo, L1_ffn_bo, L1_ffn_in_c):
    import jax
    import jax.numpy as jnp

    def _L0_attn_ref(x, ln_gamma, ln_beta, w_qkv, w_out, b_out):
        import jax, jax.numpy as jnp
        import numpy as np
        DIM = 128
        HEADS = 16
        DIM_HEAD = 64
        INNER = HEADS * DIM_HEAD

        def _attention(x, ln_gamma, ln_beta, w_qkv, w_out, b_out):
            b, n, _ = x.shape
            scale = DIM_HEAD ** (-0.5)
            mu = jnp.mean(x, axis=-1, keepdims=True)
            var = jnp.var(x, axis=-1, keepdims=True)
            xn = (x - mu) / jnp.sqrt(var + 1e-05) * ln_gamma + ln_beta
            qkv = jnp.einsum('bnd,ed->bne', xn, w_qkv)
            q, k, v = jnp.split(qkv, 3, axis=-1)
            reshape = lambda t: t.reshape(b, n, HEADS, DIM_HEAD).transpose(0, 2, 1, 3)
            q, k, v = (reshape(q) * scale, reshape(k), reshape(v))
            sim = jnp.einsum('bhid,bhjd->bhij', q, k)
            mask_value = -jnp.finfo(sim.dtype).max
            causal = jnp.triu(jnp.ones((n, n), dtype=bool), k=1)
            sim = jnp.where(causal, mask_value, sim)
            sim = sim - jax.lax.stop_gradient(jnp.max(sim, axis=-1, keepdims=True))
            attn = jax.nn.softmax(sim, axis=-1)
            out = jnp.einsum('bhij,bhjd->bhid', attn, v)
            out = out.transpose(0, 2, 1, 3).reshape(b, n, INNER)
            return jnp.einsum('bne,de->bnd', out, w_out) + b_out
        return _attention(x, ln_gamma, ln_beta, w_qkv, w_out, b_out)

    def _L0_xattn_ref(teacher_features, student_features):
        import jax, jax.numpy as jnp
        import numpy as np
        from jax import lax
        BIG = jnp.float32(1e+30)

        def _pairwise_euclidean(a, b):
            aa = jnp.sum(a * a, axis=-1)[:, None]
            bb = jnp.sum(b * b, axis=-1)[None, :]
            ab = a @ b.T
            return jnp.sqrt(jnp.maximum(aa + bb - 2.0 * ab, 0.0))

        def _dtw_cost(D):
            row0 = jnp.cumsum(D[0])

            def row_step(prev_row, d_row):
                first = d_row[0] + prev_row[0]

                def col_step(left, inp):
                    d_ij, up, diag = inp
                    r = d_ij + jnp.minimum(jnp.minimum(up, left), diag)
                    return (r, r)
                _, rest = lax.scan(col_step, first, (d_row[1:], prev_row[1:], prev_row[:-1]))
                row = jnp.concatenate([first[None], rest])
                return (row, row)
            _, rows = lax.scan(row_step, row0, D[1:])
            return jnp.concatenate([row0[None], rows], axis=0)

        def _backtrack(R, T1, T2):
            L = T1 + T2 - 1

            def step(carry, _):
                i, j, done = carry
                valid = jnp.logical_not(done)
                cd = jnp.where((i > 0) & (j > 0), R[jnp.maximum(i - 1, 0), jnp.maximum(j - 1, 0)], BIG)
                cu = jnp.where(i > 0, R[jnp.maximum(i - 1, 0), j], BIG)
                cl = jnp.where(j > 0, R[i, jnp.maximum(j - 1, 0)], BIG)
                choice = jnp.argmin(jnp.stack([cd, cu, cl]))
                ni = jnp.where(choice <= 1, i - 1, i)
                nj = jnp.where((choice == 0) | (choice == 2), j - 1, j)
                at_origin = (i == 0) & (j == 0)
                ni = jnp.where(at_origin, 0, ni)
                nj = jnp.where(at_origin, 0, nj)
                return ((ni, nj, done | at_origin), (i, j, valid))
            init = (jnp.int32(T1 - 1), jnp.int32(T2 - 1), jnp.bool_(False))
            _, (i_idx, j_idx, valid) = lax.scan(step, init, None, length=L)
            return (i_idx, j_idx, valid)

        def _align_one(small, large):
            T_small, d = small.shape
            T_large = large.shape[0]
            D = _pairwise_euclidean(small, large)
            R = _dtw_cost(D)
            i_idx, j_idx, valid = _backtrack(R, T_small, T_large)
            contrib = small[i_idx] * valid[:, None].astype(small.dtype)
            expanded = jnp.zeros((T_large, d), dtype=small.dtype).at[j_idx].add(contrib)
            return expanded
        return jax.vmap(_align_one)(teacher_features, student_features)

    def _L0_ffn_ref(x, w_gate, c_fc, c_proj):
        import jax, jax.numpy as jnp
        import numpy as np
        N_EMBD = 128
        N_EXP = 8
        TOP_K = 2
        CAPACITY = 512
        D_FF = 3 * N_EMBD
        B, T, d = x.shape
        N = B * T
        xf = x.reshape(N, d)
        scores = jax.nn.softmax(xf @ w_gate, axis=-1)
        weights, idx = jax.lax.top_k(scores, TOP_K)
        flat_e = idx.reshape(-1)
        tok = jnp.repeat(jnp.arange(N), TOP_K)
        oh = jax.nn.one_hot(flat_e, N_EXP, dtype=jnp.int32)
        pos = (jnp.cumsum(oh, axis=0) * oh).sum(-1) - 1
        valid = pos < CAPACITY
        pos_c = jnp.where(valid, pos, 0)
        vmask = valid.astype(x.dtype)[:, None]
        exp_x = jnp.zeros((N_EXP, CAPACITY, d), x.dtype)
        exp_x = exp_x.at[flat_e, pos_c].add(xf[tok] * vmask)
        h = jnp.einsum('ecd,edf->ecf', exp_x, c_fc)
        a, g = jnp.split(h, 2, axis=-1)
        h = jax.nn.silu(a) * g
        exp_out = jnp.einsum('ecf,efd->ecd', h, c_proj)
        gathered = exp_out[flat_e, pos_c]
        w = weights.reshape(-1)[:, None] * vmask
        out = (gathered * w).reshape(N, TOP_K, d).sum(axis=1)
        return out.reshape(B, T, d)

    def _L1_attn_ref(x, w_qkv, w_out, b_out, ln_gamma, ln_beta):
        import jax, jax.numpy as jnp
        import numpy as np
        HEADS = 32
        DIM_HEAD = 32
        EPS = 1e-06
        b, n, dim = x.shape
        scale = DIM_HEAD ** (-0.5)
        qkv = x @ w_qkv
        qkv = qkv.reshape(b, n, 3, HEADS, DIM_HEAD)
        qkv = jnp.transpose(qkv, (2, 0, 3, 1, 4))
        q, k, v = (qkv[0], qkv[1], qkv[2])
        dots = jnp.einsum('bhnd,bhmd->bhnm', q, k) * scale
        attn = jax.nn.softmax(dots, axis=-1)
        out = jnp.einsum('bhnm,bhmd->bhnd', attn, v)
        out = jnp.transpose(out, (0, 2, 1, 3)).reshape(b, n, HEADS * DIM_HEAD)
        out = out @ w_out + b_out
        mu = jnp.mean(out, axis=-1, keepdims=True)
        var = jnp.mean((out - mu) ** 2, axis=-1, keepdims=True)
        out = (out - mu) / jnp.sqrt(var + EPS) * ln_gamma + ln_beta
        return out

    def _L1_xattn_ref(query, key, value, Wq, bq, Wk, bk, Wv, bv, Wo, bo):
        import jax, jax.numpy as jnp
        import numpy as np
        import math
        D_MODEL = 128
        NHEAD = 16
        HEAD_DIM = D_MODEL // NHEAD
        ROPE_BASE = 10000.0

        def _rope_cos_sin(seq_len, dtype):
            inv_freq = 1.0 / ROPE_BASE ** (jnp.arange(0, HEAD_DIM, 2, dtype=jnp.float32) / HEAD_DIM)
            t = jnp.arange(seq_len, dtype=jnp.float32)
            freqs = jnp.einsum('i,j->ij', t, inv_freq)
            emb = jnp.concatenate([freqs, freqs], axis=-1)
            return (jnp.cos(emb).astype(dtype), jnp.sin(emb).astype(dtype))

        def _rotate_half(x):
            x1, x2 = jnp.split(x, 2, axis=-1)
            return jnp.concatenate([-x2, x1], axis=-1)
        B, Sq, _ = query.shape
        Sk = key.shape[1]
        q = (query @ Wq.T + bq).reshape(B, Sq, NHEAD, HEAD_DIM)
        k = (key @ Wk.T + bk).reshape(B, Sk, NHEAD, HEAD_DIM)
        v = (value @ Wv.T + bv).reshape(B, Sk, NHEAD, HEAD_DIM)
        cos, sin = _rope_cos_sin(Sq, q.dtype)
        cos = cos[None, :, None, :]
        sin = sin[None, :, None, :]
        q = q * cos + _rotate_half(q) * sin
        k = k * cos + _rotate_half(k) * sin
        scale = 1.0 / math.sqrt(HEAD_DIM)
        scores = jnp.einsum('bqhd,bkhd->bhqk', q * scale, k)
        attn = jax.nn.softmax(scores, axis=-1)
        out = jnp.einsum('bhqk,bkhd->bqhd', attn, v).reshape(B, Sq, D_MODEL)
        return out @ Wo.T + bo

    def _L1_ffn_ref(x, wf, uf, bf, wi, ui, bi, wc, uc, bc, wo, uo, bo, in_c):
        import jax, jax.numpy as jnp
        import numpy as np
        from jax import lax
        T, B, I, M, O = (32, 64, 128, 128, 128)

        def _xavier(key, shape):
            fan_out, fan_in = shape
            limit = float(np.sqrt(6.0 / (fan_in + fan_out)))
            return jax.random.uniform(key, shape, jnp.float32, -limit, limit)
        batch = x.shape[1]
        c0 = jnp.broadcast_to(in_c, (batch, in_c.shape[0]))

        def step(c, xt):
            ft = jax.nn.sigmoid(xt @ wf.T + c @ uf.T + bf)
            it = jax.nn.sigmoid(xt @ wi.T + c @ ui.T + bi)
            gt = jnp.tanh(xt @ wc.T + c @ uc.T + bc)
            c = ft * c + it * gt
            return (c, None)
        c_final, _ = lax.scan(step, c0, x)
        h = jnp.tanh(jnp.einsum('tbi,oi->tbo', x, wo) + c_final @ uo.T + bo)
        return h
    x = _layernorm(x + _L0_attn_ref(x, L0_attn_ln_gamma, L0_attn_ln_beta, L0_attn_w_qkv, L0_attn_w_out, L0_attn_b_out), axis=-1)
    x = _layernorm(x + _L0_xattn_ref(ctx_1024, x), axis=-1)
    x = _layernorm(x + _L0_ffn_ref(x, L0_ffn_w_gate, L0_ffn_c_fc, L0_ffn_c_proj), axis=-1)
    x = _layernorm(x + _L1_attn_ref(x, L1_attn_w_qkv, L1_attn_w_out, L1_attn_b_out, L1_attn_ln_gamma, L1_attn_ln_beta), axis=-1)
    x = _layernorm(x + _L1_xattn_ref(x, ctx_1024, ctx_1024, L1_xattn_Wq, L1_xattn_bq, L1_xattn_Wk, L1_xattn_bk, L1_xattn_Wv, L1_xattn_bv, L1_xattn_Wo, L1_xattn_bo), axis=-1)
    x = _layernorm(x + _L1_ffn_ref(x, L1_ffn_wf, L1_ffn_uf, L1_ffn_bf, L1_ffn_wi, L1_ffn_ui, L1_ffn_bi, L1_ffn_wc, L1_ffn_uc, L1_ffn_bc, L1_ffn_wo, L1_ffn_uo, L1_ffn_bo, L1_ffn_in_c), axis=-1)
    return x

_drawn_inputs = setup_inputs


def setup_inputs(seed=0):
    import zlib

    import numpy as np

    out = dict(_drawn_inputs(seed))
    spreads = {'L0_attn_ln_gamma': (1.0, 0.2),
     'L0_attn_ln_beta': (0.0, 0.1),
     'L1_attn_b_out': (0.0, 0.1),
     'L1_attn_ln_gamma': (1.0, 0.2),
     'L1_attn_ln_beta': (0.0, 0.1),
     'L1_xattn_bq': (0.0, 0.404),
     'L1_xattn_bk': (0.0, 0.8),
     'L1_xattn_bv': (0.0, 0.1),
     'L1_xattn_bo': (0.0, 0.1),
     'L1_ffn_bf': (0.0, 0.693),
     'L1_ffn_bi': (0.0, 0.75),
     'L1_ffn_bc': (0.0, 0.1),
     'L1_ffn_bo': (0.0, 0.1),
     'L1_ffn_in_c': (0.0, 0.8)}
    factors = {'L0_ffn_w_gate': 8.0, 'L0_ffn_c_fc': 8.0, 'L0_ffn_c_proj': 8.0}
    for name, (base, spread) in spreads.items():
        noise = np.random.default_rng([zlib.crc32(name.encode()), seed]).standard_normal(out[name].shape)
        drawn = base * np.exp(spread * noise) if base else spread * noise
        out[name] = jnp.asarray(drawn.astype(out[name].dtype))
    for name, factor in factors.items():
        out[name] = (out[name] * factor).astype(out[name].dtype)
    return out
```

```python
import math
from contextlib import ExitStack, contextmanager

import numpy as np
import concourse.bass as bass
from concourse import mybir

FP32 = mybir.dt.float32
BF16 = mybir.dt.bfloat16
ALU = mybir.AluOpType
ACT = mybir.ActivationFunctionType
AX = mybir.AxisListType

P = 128
NB = 16
D = 128
SPAN = 512
BIG = 1e30
N_EXP = 8
CAPACITY = 512
D_FF = 384
HALF = D_FF // 2


@contextmanager
def stage_semaphores(nc, stage):
    taken = []

    def sem(name):
        taken.append(nc.alloc_semaphore(name=f"{stage}_{name}"))
        return taken[-1]
    yield sem
    nc.clear_and_free_semaphores(taken)
    nc.all_engine_barrier()


def wait(eng, sem, value):
    if isinstance(value, int) and value <= 0:
        return
    eng.wait_ge(sem, value)


def exists(b):
    return not isinstance(b, int) or 0 <= b < NB


def spread(ap, shape):
    return ap.rearrange("p (n o) -> p n o", o=1).broadcast_to(shape)


def newton_rsqrt(pool, chain, y, v, t, halves):
    chain(pool.tensor_tensor(y, v, halves, op=ALU.pow))
    chain(pool.tensor_tensor(t, y, y, op=ALU.mult))
    chain(pool.tensor_tensor(t, t, v, op=ALU.mult))
    chain(pool.tensor_scalar(t, t, -0.5, 1.5, ALU.mult, ALU.add))
    chain(pool.tensor_tensor(y, y, t, op=ALU.mult))


def wait_alone(eng, sem, value, spare):
    if isinstance(value, int):
        wait(eng, sem, value)
        return
    register, started = spare
    eng.reg_mov(register, value)
    eng.wait_ge(started, 1)
    eng.wait_ge(sem, register)


def linker(eng, sem, base=0, spare=None):
    count = [0]

    def link(ins):
        count[0] += 1
        ins.then_inc(sem, 1)
        wait_alone(eng, sem, base + count[0], spare)
    return link


def attention_stage(nc, kind, x_all, xin_all, consts, weights):
    rope = kind == "rope"
    heads = {"causal": 16, "plain": 32, "rope": 16}[kind]
    dh = {"causal": 64, "plain": 32, "rope": 8}[kind]
    G = heads // 4
    rows = 128 // (4 if rope else 1)
    dv = 32 if rope else dh
    inner = heads * dv
    per_chunk = P // dv
    chunks = 4 // per_chunk
    fills = SPAN // P // chunks
    o_banks = G // fills
    last_post = 2 if kind == "plain" else 1

    if rope:
        ITEMS = [("q0", 0, 1), ("y", 2, -1), ("xt", 3, 2)]
    elif G == 4:
        ITEMS = [("q0", 0, 1), ("k0", 0, 1), ("v0", 1, 1), ("y", 2, -1),
                 ("q1", 2, 1), ("k1", 2, 1), ("v1", 3, 1), ("xt", 3, 2)]
    else:
        ITEMS = [("q0", 0, 1), ("k0", 1, 1), ("v0", 2, 1), ("y", 3, -1),
                 ("q1", 4, 1), ("k1", 5, 1), ("v1", 6, 1), ("xt", 7, 2)]
    names = [k for k, _, _ in ITEMS]
    PROBT_ON_VECTOR = {"causal": (), "plain": (), "rope": ()}[kind]
    ON_VECTOR = {"causal": ("y", "xt"), "plain": ("y",), "rope": ("y", "q0")}[kind]

    def heads_of(g):
        if rope:
            return [(32 * g, 0, 4 * g + n) for n in range(4)]
        per = 128 // dh
        return [(dh * (g % per), 4 * (g // per) + n, (4 * (g // per) + n) * per + g % per)
                for n in range(4)]

    with ExitStack() as ctx:
        def sb(name, shape, dt=FP32):
            return ctx.enter_context(nc.sbuf_tensor(f"{kind}_{name}", shape, dt))

        def pb(name):
            return ctx.enter_context(nc.psum_tensor(f"{kind}_{name}", [P, SPAN], FP32))

        sem = ctx.enter_context(stage_semaphores(nc, kind))

        def pair(name, shape):
            return [sb(f"{name}{i}", shape) for i in range(2)]

        xin = pair("xin", [P, D])
        xT = pair("xT", [P, P])
        if rope:
            qT = pair("qT", [P, P])
            qr = pair("qr", [P, 2, P])
            kT = pair("kT", [P, 4, P])
        else:
            qT = pair("qT", [P, inner])
            kT = pair("kT", [P, inner])
        v = pair("v", [P, heads, dv])
        prob = pair("prob", [P, SPAN])
        probT = pair("probT", [P, SPAN])
        negmax = sb("negmax", [P, 4, 4])
        total = sb("total", [P, 4, 4])
        share = sb("share", [P, 4, 4])
        oT = sb("oT", [P, inner])
        xres = pair("xres", [P, D])
        z = pair("z", [P, D])
        z2 = pair("z2", [P, D])
        zt = sb("zt", [P, D])
        st = sb("st", [P, 2, 6])
        mv = sb("mv", [P, 2, 2])
        mv2 = sb("mv2", [P, 2, 2])
        rs = sb("rs", [P, 1])
        rv = sb("rv", [P, 1])
        rt = sb("rt", [P, 1])

        pmm = [pb("pmm0"), pb("pmm1")]
        psc = [pb("psc0"), pb("psc1")]
        ppt = [pb("ppt0"), pb("ppt1")]
        po = [pb("po0"), pb("po1")]

        made = {k: sem(f"made_{k}") for k in names}
        moved = {k: sem(f"moved_{k}") for k in names}
        xin_ready = sem("xin_ready")
        kv_ready = sem("kv_ready")
        zeros_ready = sem("zeros_ready")
        scores_made = sem("scores_made")
        max_ready = sem("max_ready")
        prob_ready = sem("prob_ready")
        prob_turned = sem("prob_turned")
        probT_ready = [sem("probT_ready0"), sem("probT_ready1")]
        pv_made = sem("pv_made")
        share_ready = sem("share_ready")
        norm_ready = sem("norm_ready")
        o_moved = sem("o_moved")
        xres_ready = sem("xres_ready")
        z_ready = sem("z_ready")
        zst_ready = sem("zst_ready")
        stats_ready = sem("stats_ready")
        z2_ready = sem("z2_ready")
        z2st_ready = sem("z2st_ready")
        stats2_ready = sem("stats2_ready")
        qr_ready = sem("qr_ready")
        done = sem("done")
        pool_step = sem("pool_step")
        pool_step2 = sem("pool_step2")
        dve_started = sem("dve_started")
        pool_started = sem("pool_started")

        def bank_free(eng, b, n):
            at = n
            bb = b
            for _ in range(5 * len(ITEMS)):
                at -= 1
                if at < 0:
                    at += len(ITEMS)
                    bb = bb - 1
                k, _, off = ITEMS[at]
                if at % 2 == n % 2 and exists(bb + off):
                    wait(eng, moved[k], bb + off + 1)
                    return

        def bodies(eng, body):
            for b in range(-2, 2):
                body(b, b % 2)
            with eng.Fori(1, NB // 2 - 1) as i:
                for u in range(2):
                    body(i * 2 + u, u)
            for b in range(NB - 2, NB + last_post):
                body(b, b % 2)

        with nc.Block() as block:
            @block.tensor
            def _(pe):
                def scores(b, g, p, t):
                    if g == 0:
                        wait(pe, moved["q0"], b + 1)
                        wait(pe, kv_ready if rope else moved["k0"], b + 1)
                    elif g == G // 2 and not rope:
                        wait(pe, moved["q1"], b + 1)
                        wait(pe, moved["k1"], b + 1)
                    wait(pe, prob_ready, t - 1)
                    s = psc[g % 2]
                    if rope:
                        r = 32 * g
                        pe.matmul(s[:, :], qT[p][r:r + rows, :], kT[p][r:r + rows, :, :],
                                  start=True, stop=True).then_inc(scores_made, 1)
                        return
                    causal = kind == "causal"
                    if causal:
                        pe.matmul(s[:, :], consts["ident_bf"], consts["mask_bf"], start=True,
                                  stop=False, skip_group_check=True)
                    for n, (r, c, h) in enumerate(heads_of(g)):
                        mm = pe.matmul(s[:, n * P:(n + 1) * P], qT[p][r:r + dh, c * P:(c + 1) * P],
                                       kT[p][r:r + dh, c * P:(c + 1) * P], start=not causal,
                                       stop=True, skip_group_check=causal)
                    mm.then_inc(scores_made, 1)

                def item(k, b, p, bank):
                    m = pmm[bank]
                    if k == "xt":
                        wait(pe, xin_ready, b + 1)
                        mm = pe.transpose(m[:, 0:P], xin[p][:, :], consts["ident"])
                    elif k == "q0" and rope:
                        wait(pe, moved["xt"], b + 1)
                        pe.matmul(m[:, 0:P], weights["wq"], xT[p][:, :], start=True, stop=True)
                        mm = pe.matmul(m[:, P:2 * P], weights["wq_turned"], xT[p][:, :],
                                       start=True, stop=True)
                    elif k[0] in "qk":
                        wait(pe, moved["xt"], b + 1)
                        first = (0 if k[0] == "q" else inner) + int(k[1]) * SPAN
                        for n in range(4):
                            mm = pe.matmul(m[:, n * P:(n + 1) * P],
                                           weights["wqkv"][:, first + n * P:first + (n + 1) * P],
                                           xT[p][:, :], start=True, stop=True)
                    elif k[0] == "v":
                        first = 2 * inner + int(k[1]) * SPAN
                        mm = pe.matmul(m[:, :], xT[p][:, :], weights["wqkv"][:, first:first + SPAN],
                                       start=True, stop=True)
                    else:
                        wait(pe, o_moved, (b + 1) * o_banks)
                        for c in range(inner // P):
                            mm = pe.matmul(m[:, 0:P], oT[:, c * P:(c + 1) * P],
                                           weights["wo"][:, c * P:(c + 1) * P],
                                           start=c == 0, stop=c == inner // P - 1)
                    mm.then_inc(made[k], 1)

                def body(b, p):
                    for g in range(G):
                        t = b * G + g
                        bs = b + (g + 2) // G
                        if exists(bs):
                            scores(bs, (g + 2) % G, (p + (g + 2) // G) % 2, t + 2)
                        for n, (k, slot, off) in enumerate(ITEMS):
                            if slot == g and exists(b + off):
                                bank_free(pe, b, n)
                                item(k, b + off, (p + off) % 2, n % 2)
                        if exists(b):
                            wait(pe, norm_ready, t + 1)
                            wait(pe, probT_ready[g % 2], b * (G // 2) + g // 2)
                            for n in range(4):
                                mm = pe.transpose(ppt[g % 2][:, n * P:(n + 1) * P],
                                                  prob[g % 2][:, n * P:(n + 1) * P],
                                                  consts["ident"])
                            mm.then_inc(prob_turned, 1)
                        bv = b - (g == 0)
                        if exists(bv):
                            gv, pv = (g - 1) % G, (p + (g == 0)) % 2
                            if rope and gv == 0:
                                wait(pe, kv_ready, bv + 1)
                                wait(pe, zeros_ready, 2)
                            elif gv == 0:
                                wait(pe, moved["v0"], bv + 1)
                            elif gv == G // 2 and not rope:
                                wait(pe, moved["v1"], bv + 1)
                            wait(pe, probT_ready[gv % 2], bv * (G // 2) + gv // 2 + 1)
                            if gv % fills == 0:
                                wait(pe, o_moved, (bv - 1) * 2 + gv // fills + 1 if o_banks == 2 else bv - 1)
                            bank = po[gv // fills if o_banks == 2 else pv]
                            for n, (_, _, h) in enumerate(heads_of(gv)):
                                r = n % per_chunk * dv
                                c = gv % fills * chunks + n // per_chunk
                                mm = pe.matmul(bank[r:r + dv, c * P:(c + 1) * P], v[pv][:, h, :],
                                               probT[gv % 2][:, n * P:(n + 1) * P], start=True, stop=True)
                            mm.then_inc(pv_made, 1)

                bodies(pe, body)

            def move_item(eng, k, b, p, bank):
                m = pmm[bank]
                on_act = k not in ON_VECTOR
                wait(eng, made[k], b + 1)

                def copy(out, in_, scale=1.0):
                    if on_act:
                        return eng.activation(out, in_, ACT.Copy, scale=scale)
                    if scale == 1.0:
                        return eng.tensor_copy(out, in_)
                    return eng.tensor_scalar(out, in_, scale, None, ALU.mult)

                if k == "xt":
                    if kind == "causal":
                        ins = eng.tensor_scalar(xT[p][:, :], m[:, 0:P], weights["gamma_col"],
                                                weights["beta_col"], ALU.mult, ALU.add)
                    else:
                        ins = copy(xT[p][:, :], m[:, 0:P])
                elif k[0] == "q":
                    ins = copy(qT[p][:, int(k[1]) * SPAN:(int(k[1]) + 1) * SPAN], m[:, :], dh ** -0.5)
                elif k[0] == "k":
                    ins = copy(kT[p][:, int(k[1]) * SPAN:(int(k[1]) + 1) * SPAN], m[:, :])
                elif k[0] == "v":
                    nh = SPAN // dh
                    ins = copy(v[p][:, int(k[1]) * nh:(int(k[1]) + 1) * nh, 0:dh],
                               m[:, :].rearrange("p (h d) -> p h d", d=dh))
                ins.then_inc(moved[k], 1)

            @block.scalar
            def _(act):
                act.preload_act_table(ACT.Exp)

                def body(b, p):
                    for g in range(G):
                        t = b * G + g
                        be, ge = b + (g + 1) // G, (g + 1) % G
                        if exists(be):
                            wait(act, max_ready, t + 2)
                            wait(act, prob_turned, t)
                            for n in range(4):
                                ins = act.activation(prob[ge % 2][:, n * P:(n + 1) * P],
                                                     psc[ge % 2][:, n * P:(n + 1) * P], ACT.Exp,
                                                     bias=negmax[:, ge % 4, n:n + 1],
                                                     accum_out=total[:, ge % 4, n:n + 1])
                            ins.then_inc(prob_ready, 1)
                        for n, (k, slot, off) in enumerate(ITEMS):
                            if slot == g and exists(b + off) and k not in ON_VECTOR:
                                move_item(act, k, b + off, (p + off) % 2, n % 2)
                        if exists(b) and g % 2 not in PROBT_ON_VECTOR:
                            wait(act, prob_turned, t + 1)
                            wait(act, pv_made, t - 1)
                            act.activation(probT[g % 2][:, :], ppt[g % 2][:, :], ACT.Copy)\
                               .then_inc(probT_ready[g % 2], 1)

                bodies(act, body)

            @block.vector
            def _(dve):
                dve_spare = (dve.alloc_register("spare_dve_" + kind), dve_started)
                dve.engine_nop().then_inc(dve_started, 1)
                def body(b, p):
                    for g in range(G):
                        t = b * G + g
                        if exists(b):
                            wait(dve, prob_ready, t + 1)
                            dve.reciprocal(share[:, g % 4, :], total[:, g % 4, :]).then_inc(share_ready, 1)
                            wait(dve, share_ready, t + 1)
                            pr = prob[g % 2][:, :].rearrange("p (h k) -> p h k", h=4)
                            dve.tensor_tensor(pr, pr, spread(share[:, g % 4, :], [P, 4, P]), op=ALU.mult)\
                               .then_inc(norm_ready, 1)
                        bm = b + (g + 2) // G
                        if exists(bm):
                            gm = (g + 2) % G
                            wait(dve, scores_made, t + 3)
                            wait(dve, prob_ready, t - 1)
                            dve.tensor_reduce(negmax[:, gm % 4, :],
                                              psc[gm % 2][:, :].rearrange("p (h k) -> p h k", h=4),
                                              AX.X, ALU.max, negate=True).then_inc(max_ready, 1)
                        if exists(b) and g % 2 in PROBT_ON_VECTOR:
                            wait(dve, prob_turned, t + 1)
                            wait(dve, pv_made, t - 1)
                            dve.tensor_copy(probT[g % 2][:, :], ppt[g % 2][:, :])\
                               .then_inc(probT_ready[g % 2], 1)
                        for n, (k, slot, off) in enumerate(ITEMS):
                            if slot != g or not exists(b + off) or k not in ON_VECTOR:
                                continue
                            bi, pi, m = b + off, (p + off) % 2, pmm[n % 2]
                            if k == "y":
                                wait(dve, made[k], bi + 1)
                                wait(dve, xres_ready, bi + 1)
                                dve.tensor_tensor(z[pi][:, :], m[:, 0:P],
                                                  weights["bout"] if kind == "plain" else xres[pi][:, :],
                                                  op=ALU.add).then_inc(moved[k], 1)
                            elif k == "q0" and rope:
                                wait(dve, made[k], bi + 1)
                                dve.scalar_tensor_tensor(qr[pi][:, 0, :], m[:, 0:P], weights["bq"],
                                                         consts["cos_q"], ALU.add, ALU.mult)\
                                   .then_inc(qr_ready, 1)
                                dve.scalar_tensor_tensor(qr[pi][:, 1, :], m[:, P:2 * P],
                                                         weights["bq_turned"], consts["sin_q"],
                                                         ALU.add, ALU.mult).then_inc(qr_ready, 1)
                                wait(dve, qr_ready, 2 * bi + 2)
                                dve.tensor_tensor(qT[pi][:, :], qr[pi][:, 0, :], qr[pi][:, 1, :],
                                                  op=ALU.add).then_inc(moved[k], 1)
                            else:
                                move_item(dve, k, bi, pi, n % 2)
                        for half, at, back in ((0, fills + 1, 0), (1, 1, 1)) if o_banks == 2 else ((0, 1, 1),):
                            if g == at and exists(b - back):
                                bo = b - back
                                wait(dve, pv_made, bo * G + (half + 1) * fills)
                                wait(dve, made["y"], bo)
                                dve.tensor_copy(oT[:, half * SPAN:(half + 1) * SPAN],
                                                po[half if o_banks == 2 else (p + back) % 2][:, :])\
                                   .then_inc(o_moved, 1)
                        if ("y", g, -1) in ITEMS and exists(b - 1):
                            wait(dve, moved["y"], b)
                            dve.bn_stats(st[:, 0, :], z[1 - p][:, :]).then_inc(zst_ready, 1)
                            wait_alone(dve, zst_ready, b, dve_spare)
                            dve.bn_aggr(mv[:, 1 - p, :], st[:, 0, :]).then_inc(stats_ready, 1)
                        if kind == "plain" and g == 1 and exists(b - 2):
                            wait(dve, z2_ready, b - 1)
                            dve.bn_stats(st[:, 1, :], z2[p][:, :]).then_inc(z2st_ready, 1)
                            wait_alone(dve, z2st_ready, b - 1, dve_spare)
                            dve.bn_aggr(mv2[:, p, :], st[:, 1, :]).then_inc(stats2_ready, 1)

                bodies(dve, body)

            @block.gpsimd
            def _(pool):
                pool_spare = (pool.alloc_register("spare_pool_" + kind), pool_started)
                pool.engine_nop().then_inc(pool_started, 1)
                if rope:
                    for i in range(2):
                        pool.memset(v[i][:, :, dh:dv], 0.0).then_inc(zeros_ready, 1)

                def normalise(b, p, stats, zz, out, eps, link, last):
                    link(pool.tensor_scalar(rv[:, :], stats[:, p, 1:2], eps, None, ALU.add))
                    newton_rsqrt(pool, link, rs[:, :], rv[:, :], rt[:, :], consts["neg_half"][:, 0:1])
                    link(pool.tensor_scalar(zt[:, :], zz[p][:, :], stats[:, p, 0:1], None, ALU.subtract))
                    ins = pool.tensor_tensor(out, zt[:, :], rs[:, 0:1].broadcast_to([P, D]), op=ALU.mult)
                    if last:
                        ins.then_inc(last, 1)
                        wait_alone(pool, last, b + 1, pool_spare)
                    else:
                        link(ins)

                def body(b, p):
                    if exists(b + 2):
                        wait_alone(pool, made["xt"], b + 1, pool_spare)
                        pool.tensor_copy(xin[p][:, :], xin_all[:, bass.ds((b + 2) * D, D)])\
                            .then_inc(xin_ready, 1)
                    if rope and exists(b + 1):
                        q = (p + 1) % 2
                        wait_alone(pool, pv_made, b * G, pool_spare)
                        pool.tensor_tensor(kT[q][:, :, :],
                                           consts["kT_all"][:, bass.ds((b + 1) * P, P)]
                                           .rearrange("p (o k) -> p o k", o=1).broadcast_to([P, 4, P]),
                                           spread(consts["block_of"], [P, 4, P]), op=ALU.mult)
                        pool.tensor_copy(v[q][:, :, 0:dh],
                                         consts["v_all"][:, bass.ds((b + 1) * P, P)]
                                         .rearrange("p (h d) -> p h d", d=dh)).then_inc(kv_ready, 1)
                    if exists(b) and kind != "plain":
                        wait_alone(pool, moved["y"], b - 1, pool_spare)
                        pool.tensor_tensor(xres[p][:, :], x_all[:, bass.ds(b * D, D)], weights["bout"],
                                           op=ALU.add).then_inc(xres_ready, 1)
                    elif exists(b):
                        pool.tensor_copy(xres[p][:, :], x_all[:, bass.ds(b * D, D)])\
                            .then_inc(xres_ready, 1)
                    if kind == "plain" and exists(b - 2):
                        wait_alone(pool, stats2_ready, b - 1, pool_spare)
                        normalise(b - 2, p, mv2, z2, x_all[:, bass.ds((b - 2) * D, D)], 1e-5,
                                  linker(pool, pool_step2, (b - 2) * 7, pool_spare), done)
                    if exists(b - 1):
                        q = (p + 1) % 2
                        wait_alone(pool, stats_ready, b, pool_spare)
                        if kind == "plain":
                            link = linker(pool, pool_step, (b - 1) * 10, pool_spare)
                            normalise(b - 1, q, mv, z, zt[:, :], 1e-6, link, None)
                            link(pool.tensor_tensor(zt[:, :], zt[:, :], weights["gamma"], op=ALU.mult))
                            link(pool.tensor_tensor(zt[:, :], zt[:, :], weights["beta"], op=ALU.add))
                            pool.tensor_tensor(z2[q][:, :], zt[:, :], xres[q][:, :], op=ALU.add)\
                                .then_inc(z2_ready, 1)
                            wait_alone(pool, z2_ready, b, pool_spare)
                        else:
                            normalise(b - 1, q, mv, z, x_all[:, bass.ds((b - 1) * D, D)], 1e-5,
                                      linker(pool, pool_step, (b - 1) * 7, pool_spare), done)

                bodies(pool, body)


def layer_norm_all(nc, name, consts, z, x_all):
    with ExitStack() as ctx:
        def sem(n):
            return ctx.enter_context(nc.semaphore(f"{name}_ln_{n}"))

        st = ctx.enter_context(nc.sbuf_tensor(f"{name}_st", [P, NB, 6], FP32))
        mv = ctx.enter_context(nc.sbuf_tensor(f"{name}_mv", [P, NB, 2], FP32))
        rs = ctx.enter_context(nc.sbuf_tensor(f"{name}_rs", [P, 3, NB], FP32))
        stats, variances, step, applied = sem("stats"), sem("variances"), sem("step"), sem("applied")
        with nc.Block() as block:
            @block.vector
            def _(dve):
                for b in range(NB):
                    dve.bn_stats(st[:, b, :], z[:, b * D:(b + 1) * D]).then_inc(stats, 1)
                for b in range(NB):
                    dve.wait_ge(stats, b + 1)
                    dve.bn_aggr(mv[:, b, :], st[:, b, :]).then_inc(variances, 1)
                dve.wait_ge(variances, NB)
                dve.wait_ge(step, 6)
                for b in range(NB):
                    dve.tensor_scalar(x_all[:, b * D:(b + 1) * D], z[:, b * D:(b + 1) * D],
                                      mv[:, b, 0:1], rs[:, 1, b:b + 1], ALU.subtract, ALU.mult)\
                       .then_inc(applied, 1)

            @block.gpsimd
            def _(pool):
                pool.wait_ge(variances, NB)
                link = linker(pool, step)
                link(pool.tensor_scalar(rs[:, 0, :], mv[:, :, 1], 1e-5, None, ALU.add))
                newton_rsqrt(pool, link, rs[:, 1, :], rs[:, 0, :], rs[:, 2, :],
                             consts["neg_half"][:, 0:NB])


def alignment_stage(nc, consts, x_all, ctx_all, ctxT_all):
    R1 = P + 1
    ctx = ExitStack()
    with ctx:
        sem = ctx.enter_context(stage_semaphores(nc, "dtw"))

        def sb(name, shape, where=ctx):
            return where.enter_context(nc.sbuf_tensor(f"dtw_{name}", shape, FP32))

        dist_dram = nc.dram_tensor("dist_dram", [NB, P, P], FP32, kind="Internal").ap()
        cost_dram = nc.dram_tensor("cost_dram", [NB, R1, R1], FP32, kind="Internal").ap()
        jump_dram = nc.dram_tensor("jump_dram", [NB, P, P], FP32, kind="Internal").ap()

        with ExitStack() as part:
            xsq = sb("xsq", [P, NB * P], part)
            xm2 = sb("xm2", [P, NB * P], part)
            csq = sb("csq", [P, D], part)
            norm = sb("norm", [P, NB], part)
            a = sb("a", [P, NB * P], part)
            s = sb("s", [P, NB * P], part)
            sq = sb("sq", [P, NB * P], part)
            inv = sb("inv", [P, NB * P], part)
            turn = [part.enter_context(nc.psum_tensor(f"dtw_turn{i}", [P, SPAN], FP32)) for i in range(4)]
            dist = [part.enter_context(nc.psum_tensor(f"dtw_dist{i}", [P, SPAN], FP32)) for i in range(4)]
            turned, squared, doubled, norms = sem("turned"), sem("squared"), sem("doubled"), sem("norms")
            norm_step = sem("norm_step")
            dist_made, a_ready, s_ready = sem("dist_made"), sem("a_ready"), sem("s_ready")
            sq_ready, r_ready, m_ready, inv_ready = sem("sq"), sem("r"), sem("m"), sem("inv")
            fix_ready, d_ready, d_stored = sem("fix"), sem("d"), sem("d_stored")

            def chunk(t, c):
                return t[:, c * SPAN:(c + 1) * SPAN]

            with nc.Block() as block:
                @block.tensor
                def _(pe):
                    for c in range(4):
                        for m in range(4):
                            b = 4 * c + m
                            mm = pe.transpose(turn[c][:, m * P:(m + 1) * P], x_all[:, b * D:(b + 1) * D],
                                              consts["ident"])
                        mm.then_inc(turned, 1)
                    for c in range(4):
                        pe.wait_ge(squared, c + 1)
                        pe.matmul(dist[c][:, :], consts["ones"], chunk(xsq, c), start=True,
                                  stop=False, skip_group_check=True)
                        pe.wait_ge(doubled, c + 1)
                        for m in range(4):
                            b = 4 * c + m
                            mm = pe.matmul(dist[c][:, m * P:(m + 1) * P], ctxT_all[:, b * P:(b + 1) * P],
                                           xm2[:, b * P:(b + 1) * P], start=False, stop=True,
                                           skip_group_check=True)
                        mm.then_inc(dist_made, 1)

                @block.scalar
                def _(act):
                    for c in range(4):
                        act.wait_ge(turned, c + 1)
                        act.activation(chunk(xsq, c), turn[c][:, :], ACT.Square).then_inc(squared, 1)
                    for b in range(NB):
                        wait(act, norm_step, b)
                        act.activation(csq[:, :], ctx_all[:, b * D:(b + 1) * D], ACT.Square,
                                       accum_out=norm[:, b:b + 1]).then_inc(norm_step, 1)
                    act.preload_act_table(ACT.Sqrt)
                    for c in range(4):
                        act.wait_ge(a_ready, 4 * c + 4)
                        act.activation(chunk(s, c), chunk(a, c), ACT.Sqrt).then_inc(s_ready, 1)

                @block.vector
                def _(dve):
                    for c in range(4):
                        dve.wait_ge(turned, c + 1)
                        dve.wait_ge(squared, c + 1)
                        dve.tensor_scalar(chunk(xm2, c), turn[c][:, :], -2.0, None, ALU.mult)\
                           .then_inc(doubled, 1)
                    dve.wait_ge(norm_step, NB)
                    for c in range(4):
                        dve.wait_ge(dist_made, c + 1)
                        for m in range(4):
                            b = 4 * c + m
                            dve.tensor_scalar(a[:, b * P:(b + 1) * P], dist[c][:, m * P:(m + 1) * P],
                                              norm[:, b:b + 1], 0.0, ALU.add, ALU.max).then_inc(a_ready, 1)
                    for c in range(4):
                        dve.wait_ge(s_ready, c + 1)
                        dve.tensor_scalar(chunk(inv, c), chunk(s, c), 1e-18, None, ALU.max)\
                           .then_inc(m_ready, 1)
                        dve.wait_ge(m_ready, c + 1)
                        dve.reciprocal(chunk(inv, c), chunk(inv, c)).then_inc(inv_ready, 1)
                        dve.wait_ge(inv_ready, c + 1)
                        dve.wait_ge(r_ready, c + 1)
                        dve.scalar_tensor_tensor(chunk(inv, c), chunk(sq, c), 0.5, chunk(inv, c),
                                                 ALU.mult, ALU.mult).then_inc(fix_ready, 1)
                        dve.wait_ge(fix_ready, c + 1)
                        dve.tensor_tensor(chunk(a, c), chunk(s, c), chunk(inv, c), op=ALU.add)\
                           .then_inc(d_ready, 1)

                @block.gpsimd
                def _(pool):
                    for c in range(4):
                        pool.wait_ge(s_ready, c + 1)
                        pool.tensor_tensor(chunk(sq, c), chunk(s, c), chunk(s, c), op=ALU.mult)\
                            .then_inc(sq_ready, 1)
                        pool.wait_ge(sq_ready, c + 1)
                        pool.tensor_tensor(chunk(sq, c), chunk(a, c), chunk(sq, c), op=ALU.subtract)\
                            .then_inc(r_ready, 1)

                @block.sync
                def _(sp):
                    for c in range(4):
                        sp.wait_ge(d_ready, c + 1)
                        sp.dma_start(dist_dram[4 * c:4 * c + 4].rearrange("b i j -> i b j"),
                                     chunk(a, c).rearrange("i (b j) -> i b j", b=4)).then_inc(d_stored, 16)
                    sp.wait_ge(d_stored, 64)

        with ExitStack() as part:
            cost = sb("cost", [NB, R1 * R1], part)
            low = [sb(f"low{i}", [NB, P], part) for i in range(2)]
            rows = cost[:, :].rearrange("b (i j) -> b i j", j=R1)
            d_loaded, edges = sem("d_loaded"), sem("edges")
            low_ready, row_ready, cost_stored = sem("low_ready"), sem("row_ready"), sem("cost_stored")
            with nc.Block() as block:
                @block.sync
                def _(sp):
                    sp.dma_start(rows[:, 1:R1, 1:R1], dist_dram).then_inc(d_loaded, 16)
                    sp.wait_ge(row_ready, P)
                    sp.wait_ge(edges, 3)
                    sp.dma_start(cost_dram.rearrange("b i j -> b (i j)"), cost[:, :])\
                      .then_inc(cost_stored, 16)
                    sp.wait_ge(cost_stored, 16)

                @block.vector
                def _(dve):
                    dve.memset(rows[:, 0, :], BIG).then_inc(edges, 1)
                    dve.memset(rows[:, 1:R1, 0:1], BIG).then_inc(edges, 1)
                    dve.memset(low[0][:, :], BIG).then_inc(edges, 1)
                    dve.wait_ge(edges, 3)
                    dve.wait_ge(d_loaded, 16)

                    def row(i, p, first=False):
                        at = (i + 1) * R1
                        if not first:
                            wait(dve, row_ready, i)
                            dve.tensor_tensor(low[p][:, :], cost[:, i * R1 + 1:(i + 1) * R1],
                                              cost[:, i * R1:i * R1 + P], op=ALU.min)\
                               .then_inc(low_ready, 1)
                            wait(dve, low_ready, i)
                        here = cost[:, at + 1:at + R1]
                        dve.tensor_tensor_scan(here, low[p][:, :], here, 0.0 if first else BIG,
                                               ALU.min, ALU.add).then_inc(row_ready, 1)

                    for i in range(P):
                        row(i, i % 2, first=i == 0)

        jump = sb("jump", [P, NB * P])
        last = sb("last", [P, NB * P])
        col = sb("col", [P, NB * P])
        with ExitStack() as part:
            here = sb("here", [P, NB, R1], part)
            above = sb("above", [P, NB, R1], part)
            low = sb("lowest", [P, NB, P], part)
            leaves = sb("leaves", [P, NB, P], part)
            diag = sb("diag", [P, NB, P], part)
            cost_loaded, col_ready, step = sem("cost_loaded"), sem("col_ready"), sem("choice_step")
            jump_ready, jump_stored = sem("jump_ready"), sem("jump_stored")
            with nc.Block() as block:
                @block.sync
                def _(sp):
                    sp.dma_start(here[:, :, :], cost_dram[:, 1:R1, :].rearrange("b i j -> i b j"))\
                      .then_inc(cost_loaded, 16)
                    sp.wait_ge(jump_ready, 1)
                    sp.dma_start(jump_dram.rearrange("b i j -> i b j"),
                                 jump[:, :].rearrange("i (b j) -> i b j", b=NB)).then_inc(jump_stored, 16)
                    sp.wait_ge(jump_stored, 16)

                @block.scalar
                def _(act):
                    act.dma_start(above[:, :, :], cost_dram[:, 0:P, :].rearrange("b i j -> i b j"))\
                       .then_inc(cost_loaded, 16)
                    act.wait_ge(cost_loaded, 32)

                @block.gpsimd
                def _(pool):
                    pool.iota(col[:, :].rearrange("p (b j) -> p b j", b=NB), pattern=[[256, NB], [1, P]],
                              base=1, channel_multiplier=0,
                              allow_small_or_imprecise_dtypes=True).then_inc(col_ready, 1)

                @block.vector
                def _(dve):
                    link = linker(dve, step)
                    col3 = col[:, :].rearrange("p (b j) -> p b j", b=NB)
                    up, corner, left = above[:, :, 1:R1], above[:, :, 0:P], here[:, :, 0:P]
                    dve.wait_ge(cost_loaded, 32)
                    dve.tensor_tensor(diag[:, :, :], corner, up, op=ALU.is_le).then_inc(step, 1)
                    dve.tensor_tensor(low[:, :, :], corner, up, op=ALU.min).then_inc(step, 1)
                    dve.wait_ge(step, 2)
                    dve.tensor_tensor(leaves[:, :, :], low[:, :, :], left, op=ALU.is_le).then_inc(step, 1)
                    dve.wait_ge(step, 3)
                    dve.wait_ge(col_ready, 1)
                    dve.tensor_tensor(leaves[:, :, :], leaves[:, :, :], col3, op=ALU.mult).then_inc(step, 1)
                    dve.wait_ge(step, 4)
                    dve.tensor_tensor(low[:, :, :], leaves[:, :, :], diag[:, :, :], op=ALU.subtract)\
                       .then_inc(step, 1)
                    dve.wait_ge(step, 5)
                    n = low[:, :, :].rearrange("p b j -> p (b j)")
                    l = leaves[:, :, :].rearrange("p b j -> p (b j)")
                    dve.tensor_tensor_scan(jump[:, :], n, n, 0.0, ALU.max, ALU.max).then_inc(jump_ready, 1)
                    dve.tensor_tensor_scan(last[:, :], l, l, 0.0, ALU.max, ALU.max).then_inc(step, 1)

        enter = sb("enter", [NB, P])
        with ExitStack() as part:
            table = sb("table", [NB, P * P], part)
            junk = sb("junk", [NB, P], part)
            col_b = sb("col_b", [NB, P], part)
            table_loaded, col_ready, entered = sem("table_loaded"), sem("col_b_ready"), sem("entered")
            with nc.Block() as block:
                @block.sync
                def _(sp):
                    sp.dma_start(table[:, :], jump_dram.rearrange("b i j -> b (i j)"))\
                      .then_inc(table_loaded, 16)

                @block.gpsimd
                def _(pool):
                    pool.iota(col_b[:, :], pattern=[[1, P]], base=1, channel_multiplier=256,
                              allow_small_or_imprecise_dtypes=True).then_inc(col_ready, 1)

                @block.vector
                def _(dve):
                    dve.wait_ge(col_ready, 1)
                    dve.tensor_copy(enter[:, P - 1:P], col_b[:, P - 1:P]).then_inc(entered, 1)
                    dve.wait_ge(table_loaded, 16)

                    def step(k):
                        wait(dve, entered, k + 1)
                        i = P - 1 - k
                        dve.scalar_tensor_tensor(junk[:, :], col_b[:, :], enter[:, i:i + 1],
                                                 table[:, i * P:(i + 1) * P], ALU.is_equal, ALU.mult,
                                                 accum_out=enter[:, i - 1:i])\
                           .then_inc(entered, 1)

                    for k in range(P - 1):
                        step(k)

        with ExitStack() as part:
            hi = sb("hi", [P, NB], part)
            lo = sb("lo", [P, NB], part)
            junk = sb("junk5", [P, NB * P], part)
            below = sb("below", [P, NB * P], part)
            z = sb("z", [P, NB * D], part)
            hi_bank = part.enter_context(nc.psum_tensor("dtw_hi_bank", [P, SPAN], FP32))
            add = [part.enter_context(nc.psum_tensor(f"dtw_add{i}", [P, SPAN], FP32)) for i in range(4)]
            hi_made, hi_ready, lo_ready = sem("hi_made"), sem("hi_ready"), sem("lo_ready")
            below_ready, above_ready, path_ready = sem("below_ready"), sem("above_ready"), sem("path_ready")
            added, z_ready = sem("added"), sem("z_ready")

            def wide(t, n):
                return spread(t[:, :], [P, NB, n])

            with nc.Block() as block:
                @block.tensor
                def _(pe):
                    pe.matmul(hi_bank[:, 0:NB], enter[:, :], consts["ident"][0:NB, 0:NB], start=True,
                              stop=True).then_inc(hi_made, 1)
                    for c in range(4):
                        pe.wait_ge(path_ready, c + 1)
                        for m in range(4):
                            b = 4 * c + m
                            mm = pe.matmul(add[c][:, m * D:(m + 1) * D], junk[:, b * P:(b + 1) * P],
                                           ctx_all[:, b * D:(b + 1) * D], start=True, stop=True)
                        mm.then_inc(added, 1)

                @block.vector
                def _(dve):
                    dve.wait_ge(hi_made, 1)
                    dve.tensor_copy(hi[:, :], hi_bank[:, 0:NB]).then_inc(hi_ready, 1)
                    dve.wait_ge(hi_ready, 1)
                    for b in range(NB):
                        dve.scalar_tensor_tensor(junk[:, b * P:(b + 1) * P], col[:, b * P:(b + 1) * P],
                                                 hi[:, b:b + 1], last[:, b * P:(b + 1) * P],
                                                 ALU.is_equal, ALU.mult, accum_out=lo[:, b:b + 1])\
                           .then_inc(lo_ready, 1)
                    for c in range(4):
                        cols, bs = slice(c * SPAN, (c + 1) * SPAN), slice(4 * c, 4 * c + 4)
                        col3 = col[:, cols].rearrange("p (b j) -> p b j", b=4)
                        dve.tensor_tensor(below[:, cols].rearrange("p (b j) -> p b j", b=4), col3,
                                          spread(hi[:, bs], [P, 4, P]), op=ALU.is_le)\
                           .then_inc(below_ready, 1)
                        dve.wait_ge(lo_ready, NB)
                        dve.tensor_tensor(junk[:, cols].rearrange("p (b j) -> p b j", b=4), col3,
                                          spread(lo[:, bs], [P, 4, P]), op=ALU.is_ge)\
                           .then_inc(above_ready, 1)
                        dve.wait_ge(below_ready, c + 1)
                        dve.wait_ge(above_ready, c + 1)
                        dve.tensor_tensor(junk[:, cols], junk[:, cols], below[:, cols], op=ALU.mult)\
                           .then_inc(path_ready, 1)
                    for c in range(4):
                        dve.wait_ge(added, c + 1)
                        dve.tensor_tensor(z[:, c * SPAN:(c + 1) * SPAN], add[c][:, :],
                                          x_all[:, c * SPAN:(c + 1) * SPAN], op=ALU.add).then_inc(z_ready, 1)

            layer_norm_all(nc, "dtw", consts, z, x_all)


def turn_all(nc, name, consts, x_all, xT_all):
    with ExitStack() as ctx:
        banks = [ctx.enter_context(nc.psum_tensor(f"{name}_turn{i}", [P, SPAN], FP32)) for i in range(4)]
        turned = ctx.enter_context(nc.semaphore(f"{name}_turned"))
        moved = ctx.enter_context(nc.semaphore(f"{name}_moved"))
        with nc.Block() as block:
            @block.tensor
            def _(pe):
                for b in range(NB):
                    mm = pe.transpose(banks[b // 4][:, b % 4 * P:(b % 4 + 1) * P],
                                      x_all[:, b * D:(b + 1) * D], consts["ident"])
                    if b % 4 == 3:
                        mm.then_inc(turned, 1)

            @block.scalar
            def _(act):
                for c in (0, 2):
                    act.wait_ge(turned, c + 1)
                    act.activation(xT_all[:, c * SPAN:(c + 1) * SPAN], banks[c][:, :], ACT.Copy)\
                       .then_inc(moved, 1)

            @block.vector
            def _(dve):
                for c in (1, 3):
                    dve.wait_ge(turned, c + 1)
                    dve.tensor_copy(xT_all[:, c * SPAN:(c + 1) * SPAN], banks[c][:, :]).then_inc(moved, 1)


def experts_stage(nc, consts, weights, x_all):
    with ExitStack() as ctx:
        sem = ctx.enter_context(stage_semaphores(nc, "moe"))

        def sb(name, shape, dt=FP32):
            return ctx.enter_context(nc.sbuf_tensor(f"moe_{name}", shape, dt))

        xT = sb("xT", [P, NB * P])
        turn_all(nc, "moe", consts, x_all, xT)
        GE = NB * N_EXP
        gate = sb("gate", [P, NB, N_EXP])
        z = sb("z", [P, NB * D])

        with ExitStack() as part:
            def pb(name, shape, dt=FP32):
                return part.enter_context(nc.sbuf_tensor(f"gate_{name}", shape, dt))

            logits = part.enter_context(nc.psum_tensor("gate_logits", [P, SPAN], FP32))
            place = part.enter_context(nc.psum_tensor("gate_place", [P, SPAN], FP32))
            top = pb("top", [P, NB])
            e = pb("e", [P, NB, N_EXP])
            total = pb("total", [P, NB])
            best = pb("best", [P, NB, 8])
            index = pb("index", [P, NB, 8], mybir.dt.uint32)
            chosen = pb("chosen", [P, NB, 8])
            one = pb("one", [P, 2, NB, N_EXP])
            picks = pb("picks", [P, NB, N_EXP])
            before = pb("before", [P, NB, N_EXP])
            fits = pb("fits", [P, NB, N_EXP])
            logits_made, shifted, exped, step = sem("logits"), sem("shifted"), sem("exped"), sem("step")
            placed = sem("placed")
            logits3 = logits[:, 0:GE].rearrange("p (b e) -> p b e", b=NB)

            with nc.Block() as block:
                @block.tensor
                def _(pe):
                    for b in range(NB):
                        mm = pe.matmul(logits[:, b * N_EXP:(b + 1) * N_EXP], xT[:, b * P:(b + 1) * P],
                                       weights["L0_ffn_w_gate"][:, :], start=True, stop=True)
                    mm.then_inc(logits_made, 1)
                    pe.wait_ge(shifted, 2)
                    pe.matmul(place[:, 0:GE], consts["before"], picks[:, :, :], start=True, stop=False)
                    pe.matmul(place[:, 0:GE], consts["ones"], before[:, :, :], start=False, stop=True)\
                      .then_inc(placed, 1)

                @block.scalar
                def _(act):
                    act.preload_act_table(ACT.Exp)
                    act.wait_ge(shifted, 1)
                    act.activation(e[:, :, :], e[:, :, :], ACT.Exp).then_inc(exped, 1)

                @block.vector
                def _(dve):
                    link = linker(dve, step)
                    dve.wait_ge(logits_made, 1)
                    link(dve.tensor_reduce(top[:, :], logits3, AX.X, ALU.max))
                    dve.tensor_tensor(e[:, :, :], logits3, spread(top[:, :], [P, NB, N_EXP]),
                                      op=ALU.subtract).then_inc(shifted, 1)
                    dve.wait_ge(exped, 1)
                    link(dve.tensor_reduce(total[:, :], e[:, :, :], AX.X, ALU.add))
                    link(dve.reciprocal(total[:, :], total[:, :]))
                    link(dve.tensor_tensor(e[:, :, :], e[:, :, :], spread(total[:, :], [P, NB, N_EXP]),
                                           op=ALU.mult))
                    for b in range(NB):
                        ins = dve.max(best[:, b, :], e[:, b, :])
                    link(ins)
                    for b in range(NB):
                        ins = dve.max_index(index[:, b, :], best[:, b, :], e[:, b, :])
                    link(ins)
                    link(dve.tensor_copy(chosen[:, :, :], index[:, :, :]))
                    for k in range(2):
                        ins = dve.tensor_tensor(one[:, k, :, :],
                                                consts["iota8"].rearrange("p (o e) -> p o e", o=1)
                                                .broadcast_to([P, NB, N_EXP]),
                                                chosen[:, :, k:k + 1].broadcast_to([P, NB, N_EXP]),
                                                op=ALU.is_equal)
                    link(ins)
                    link(dve.tensor_tensor(picks[:, :, :], one[:, 0, :, :], one[:, 1, :, :], op=ALU.add))
                    link(dve.memset(before[:, 0, :], 0.0))
                    for b in range(1, NB):
                        link(dve.tensor_tensor(before[:, b, :], before[:, b - 1, :], picks[:, b - 1, :],
                                               op=ALU.add))
                    dve.engine_nop().then_inc(shifted, 1)
                    link(dve.tensor_tensor(e[:, :, :], e[:, :, :], picks[:, :, :], op=ALU.mult))
                    dve.wait_ge(placed, 1)
                    link(dve.tensor_scalar(fits[:, :, :], place[:, 0:GE].rearrange("p (b e) -> p b e", b=NB),
                                           float(CAPACITY), None, ALU.is_lt))
                    link(dve.tensor_tensor(gate[:, :, :], e[:, :, :], fits[:, :, :], op=ALU.mult))

        with ExitStack() as part:
            up = [[part.enter_context(nc.psum_tensor(f"moe_{n}{u}", [P, SPAN], FP32)) for n in "ag"]
                  for u in range(3)]
            down = [part.enter_context(nc.psum_tensor(f"moe_down{e}", [P, SPAN], FP32)) for e in range(2)]
            act_a = [part.enter_context(nc.sbuf_tensor(f"moe_act{u}", [P, SPAN], FP32)) for u in range(3)]
            h = [[part.enter_context(nc.sbuf_tensor(f"moe_h{p}{u}", [P, SPAN], FP32)) for u in range(3)]
                 for p in range(2)]
            unit_made, silu_ready, h_ready = sem("unit_made"), sem("silu_ready"), sem("h_ready")
            down_made, summed = sem("down_made"), sem("summed")
            PAIRS = N_EXP // 2
            fc = weights["L0_ffn_c_fc"]
            gate2 = gate[:, :, :].rearrange("p b e -> p (b e)")

            def turns(eng, turn):
                for pair in range(PAIRS):
                    turn(0, pair, pair > 0, True)
                with eng.Fori(1, NB // 4) as c:
                    for pair in range(PAIRS):
                        turn(c, pair, True, True)
                turn(NB // 4, 0, True, False)

            with nc.Block() as block:
                @block.tensor
                def _(pe):
                    def columns(pair, u, half):
                        at = half * HALF
                        if u < 2:
                            e = 2 * pair + u
                            return fc[:, e * D_FF + at:e * D_FF + at + P]
                        at = (2 * pair + half) * P
                        return weights["fc_last"][:, at:at + P]

                    def turn(c, pair, earlier, present):
                        k = c * PAIRS + pair
                        if present:
                            for u in range(3):
                                wait(pe, h_ready, 3 * k + u - 2)
                                for half in range(2):
                                    mm = pe.matmul(up[u][half][:, :], columns(pair, u, half),
                                                   xT[:, bass.ds(c * SPAN, SPAN)], start=True, stop=True)
                                mm.then_inc(unit_made, 1)
                        if earlier:
                            before, p = (pair - 1) % PAIRS, (pair - 1) % 2
                            wait(pe, h_ready, 3 * k)
                            for e in range(2):
                                wait(pe, summed, (k - 2) * 8 + (e + 1) * 4)
                                first = weights["proj_first"][:, (2 * before + e) * D:(2 * before + e + 1) * D]
                                last = weights["proj_last"][64 * e:64 * e + 64, before * D:(before + 1) * D]
                                for m in range(4):
                                    cols = slice(m * P, (m + 1) * P)
                                    pe.matmul(down[e][:, cols], h[p][e][:, cols], first,
                                              start=True, stop=False)
                                    mm = pe.matmul(down[e][:, cols], h[p][2][64 * e:64 * e + 64, cols],
                                                   last, start=False, stop=True)
                                mm.then_inc(down_made, 1)

                    turns(pe, turn)

                @block.scalar
                def _(act):
                    act.preload_act_table(ACT.Silu)

                    def turn(c, pair, earlier, present):
                        k = c * PAIRS + pair
                        if present:
                            for u in range(3):
                                wait(act, unit_made, 3 * k + u + 1)
                                act.activation(act_a[u][:, :], up[u][0][:, :], ACT.Silu)\
                                   .then_inc(silu_ready, 1)

                    turns(act, turn)

                @block.vector
                def _(dve):
                    def turn(c, pair, earlier, present):
                        k = c * PAIRS + pair
                        if present:
                            for u in range(3):
                                wait(dve, silu_ready, 3 * k + u + 1)
                                wait(dve, down_made, 2 * k - 2)
                                dve.tensor_tensor(h[pair % 2][u][:, :], act_a[u][:, :], up[u][1][:, :],
                                                  op=ALU.mult).then_inc(h_ready, 1)
                        if earlier:
                            before = (pair - 1) % PAIRS
                            cb = c if pair else c - 1
                            for e in range(2):
                                wait(dve, down_made, 2 * k - 1 + e)
                                for m in range(4):
                                    b = cb * 4 + m
                                    zb = z[:, bass.ds(b * D, D)]
                                    base = x_all[:, bass.ds(b * D, D)] if before + e == 0 else zb
                                    if before + e > 0:
                                        wait(dve, summed, (k - 1) * 8 + e * 4 + m - 3)
                                    dve.scalar_tensor_tensor(
                                        zb, down[e][:, m * D:(m + 1) * D],
                                        gate2[:, bass.ds(b * N_EXP + 2 * before + e, 1)], base,
                                        ALU.mult, ALU.add).then_inc(summed, 1)

                    turns(dve, turn)

        layer_norm_all(nc, "moe", consts, z, x_all)


def context_keys(nc, consts, weights, ctxT_all, turned, kT_all, v_all):
    with ExitStack() as ctx:
        sem = ctx.enter_context(stage_semaphores(nc, "keys"))

        k_banks = [[ctx.enter_context(nc.psum_tensor(f"keys_k{i}{n}", [P, SPAN], FP32)) for n in range(2)]
                   for i in range(2)]
        v_banks = [ctx.enter_context(nc.psum_tensor(f"keys_v{i}", [P, SPAN], FP32)) for i in range(4)]
        rot = [ctx.enter_context(nc.sbuf_tensor(f"keys_rot{i}", [P, 2, SPAN], FP32)) for i in range(2)]
        swapped, k_made, v_made = sem("swapped"), sem("k_made"), sem("v_made")
        products, k_ready, v_ready = sem("products"), sem("k_ready"), sem("v_ready")
        v4 = v_all[:, :].rearrange("p (b h d) -> p b h d", b=NB, h=16)
        with nc.Block() as block:
            @block.scalar
            def _(act):
                for n, name in enumerate(("L1_xattn_Wk", "L1_xattn_Wq")):
                    src = weights[name][:, :].rearrange("p (h s d) -> p h s d", h=16, s=2)
                    dst = turned[n].rearrange("p (h s d) -> p h s d", h=16, s=2)
                    for half in range(2):
                        act.activation(dst[:, :, half, :], src[:, :, 1 - half, :], ACT.Copy)\
                           .then_inc(swapped, 1)

            @block.tensor
            def _(pe):
                for c in range(4):
                    cols = ctxT_all[:, c * SPAN:(c + 1) * SPAN]
                    wait(pe, k_ready, c - 1)
                    if c == 0:
                        pe.wait_ge(swapped, 2)
                    pe.matmul(k_banks[c % 2][0][:, :], weights["L1_xattn_Wk"][:, :], cols, start=True,
                              stop=True)
                    pe.matmul(k_banks[c % 2][1][:, :], turned[0], cols, start=True, stop=True)\
                      .then_inc(k_made, 1)
                    for m in range(4):
                        b = 4 * c + m
                        mm = pe.matmul(v_banks[c][:, m * P:(m + 1) * P], ctxT_all[:, b * P:(b + 1) * P],
                                       weights["L1_xattn_Wv"][:, :], start=True, stop=True)
                    mm.then_inc(v_made, 1)

            @block.vector
            def _(dve):
                def by_batch(t):
                    return t.rearrange("p (o j) -> p o j", o=1).broadcast_to([P, 4, P])

                for c in range(4):
                    dve.wait_ge(k_made, c + 1)
                    for n, (bias, table) in enumerate((("L1_xattn_bk", "cos"), ("L1_xattn_bk_turned", "sin"))):
                        dve.scalar_tensor_tensor(rot[c % 2][:, n, :].rearrange("p (b j) -> p b j", b=4),
                                                 k_banks[c % 2][n][:, :].rearrange("p (b j) -> p b j", b=4),
                                                 weights[bias], by_batch(consts[table]),
                                                 ALU.add, ALU.mult).then_inc(products, 1)
                    dve.wait_ge(products, 2 * c + 2)
                    dve.tensor_tensor(kT_all[:, c * SPAN:(c + 1) * SPAN], rot[c % 2][:, 0, :],
                                      rot[c % 2][:, 1, :], op=ALU.add).then_inc(k_ready, 1)
                    dve.wait_ge(v_made, c + 1)
                    for m in range(4):
                        dve.tensor_tensor(v4[:, 4 * c + m, :, :],
                                          v_banks[c][:, m * P:(m + 1) * P].rearrange("p (h d) -> p h d", h=16),
                                          weights["L1_xattn_bv"].rearrange("p (h d) -> p h d", h=16),
                                          op=ALU.add).then_inc(v_ready, 1)


def recurrent_stage(nc, consts, weights, x_all, xT):
    with ExitStack() as ctx:
        sem = ctx.enter_context(stage_semaphores(nc, "rnn"))

        def sb(name, shape):
            return ctx.enter_context(nc.sbuf_tensor(f"rnn_{name}", shape, FP32))

        z = sb("z", [P, NB * D])
        c_state = [sb(f"c{i}", [P, P]) for i in range(2)]
        gates = [sb(f"gates{i}", [P, 3, P]) for i in range(2)]
        parts = [sb(f"parts{i}", [P, 2, P]) for i in range(2)]
        common = sb("common", [P, D])
        hidden = sb("hidden", [P, NB * D])
        banks = [[ctx.enter_context(nc.psum_tensor(f"rnn_b{i}{n}", [P, SPAN], FP32)) for n in range(3)]
                 for i in range(2)]
        outs = [ctx.enter_context(nc.psum_tensor(f"rnn_o{i}", [P, SPAN], FP32)) for i in range(2)]
        gates_made, gates_ready, products, c_ready = sem("gates_made"), sem("gates_ready"), sem("products"), sem("c_ready")
        out_made, out_moved, tanh_ready, z_ready = sem("out_made"), sem("out_moved"), sem("tanh"), sem("z")
        W = ("wf", "wi", "wc")
        U = ("uf", "ui", "uc")
        with nc.Block() as block:
            @block.tensor
            def _(pe):
                def step(t, p, first=False):
                    for n in range(3):
                        if not first:
                            wait(pe, gates_ready, 3 * (t - 2) + n + 1)
                        pe.matmul(banks[p][n][:, 0:P], weights["L1_ffn_" + W[n]][:, :],
                                  xT[:, bass.ds(t * P, P)], start=True, stop=False)
                    wait(pe, c_ready, t + 1)
                    for n in range(3):
                        pe.matmul(banks[p][n][:, 0:P], weights["L1_ffn_" + U[n]][:, :],
                                  c_state[p][:, :], start=False, stop=True).then_inc(gates_made, 1)

                for t in range(2):
                    step(t, t, first=True)
                with pe.Fori(1, NB // 2) as k:
                    for u in range(2):
                        step(k * 2 + u, u)
                pe.wait_ge(c_ready, NB + 1)
                pe.matmul(outs[0][:, 0:D], c_state[0][:, :], weights["L1_ffn_uo"][:, :], start=True,
                          stop=True).then_inc(out_made, 1)
                for c in range(4):
                    wait(pe, out_moved, c)
                    for m in range(4):
                        b = 4 * c + m
                        mm = pe.matmul(outs[1 - c % 2][:, m * D:(m + 1) * D], xT[:, b * P:(b + 1) * P],
                                       weights["L1_ffn_wo"][:, :], start=True, stop=True)
                    mm.then_inc(out_made, 1)

            @block.scalar
            def _(act):
                act.preload_act_table_set("sigmoid_and_others")

                def step(t, p):
                    for n, (func, bias) in enumerate(((ACT.Sigmoid, "bf"), (ACT.Sigmoid, "bi"), (ACT.Tanh, "bc"))):
                        wait(act, gates_made, 3 * t + n + 1)
                        act.activation(gates[p][:, n, :], banks[p][n][:, 0:P], func,
                                       bias=weights["L1_ffn_" + bias]).then_inc(gates_ready, 1)

                for t in range(2):
                    step(t, t)
                with act.Fori(1, NB // 2) as k:
                    for u in range(2):
                        step(k * 2 + u, u)
                for c in range(4):
                    act.wait_ge(out_moved, c + 2)
                    act.activation(hidden[:, c * SPAN:(c + 1) * SPAN], z[:, c * SPAN:(c + 1) * SPAN],
                                   ACT.Tanh).then_inc(tanh_ready, 1)

            @block.vector
            def _(dve):
                dve.tensor_copy(c_state[0][:, :], weights["L1_ffn_in_c"].broadcast_to([P, P]))\
                   .then_inc(c_ready, 1)

                def step(t, p):
                    wait(dve, c_ready, t + 1)
                    wait(dve, gates_ready, 3 * t + 1)
                    dve.tensor_tensor(parts[p][:, 0, :], gates[p][:, 0, :], c_state[p][:, :], op=ALU.mult)\
                       .then_inc(products, 1)
                    wait(dve, gates_ready, 3 * t + 3)
                    dve.tensor_tensor(parts[p][:, 1, :], gates[p][:, 1, :], gates[p][:, 2, :], op=ALU.mult)\
                       .then_inc(products, 1)
                    wait(dve, products, 2 * t + 2)
                    dve.tensor_tensor(c_state[1 - p][:, :], parts[p][:, 0, :], parts[p][:, 1, :], op=ALU.add)\
                       .then_inc(c_ready, 1)

                for t in range(2):
                    step(t, t)
                with dve.Fori(1, NB // 2) as k:
                    for u in range(2):
                        step(k * 2 + u, u)
                dve.wait_ge(out_made, 1)
                dve.tensor_tensor(common[:, :], outs[0][:, 0:D], weights["L1_ffn_bo"], op=ALU.add)\
                   .then_inc(out_moved, 1)
                dve.wait_ge(out_moved, 1)
                for c in range(4):
                    dve.wait_ge(out_made, c + 2)
                    dve.tensor_tensor(z[:, c * SPAN:(c + 1) * SPAN].rearrange("p (b d) -> p b d", b=4),
                                      outs[1 - c % 2][:, :].rearrange("p (b d) -> p b d", b=4),
                                      common[:, :].rearrange("p (o d) -> p o d", o=1)
                                      .broadcast_to([P, 4, D]), op=ALU.add).then_inc(out_moved, 1)
                for c in range(4):
                    dve.wait_ge(tanh_ready, c + 1)
                    dve.tensor_tensor(z[:, c * SPAN:(c + 1) * SPAN], hidden[:, c * SPAN:(c + 1) * SPAN],
                                      x_all[:, c * SPAN:(c + 1) * SPAN], op=ALU.add).then_inc(z_ready, 1)

        layer_norm_all(nc, "rnn", consts, z, x_all)


TURNED = [("L0_attn_w_qkv", 24, "rows"), ("L0_attn_w_out", 8, "cols"),
          ("L1_xattn_Wq", 1, "rows"), ("L1_xattn_Wk", 1, "rows"), ("L1_xattn_Wv", 1, "rows"),
          ("L1_xattn_Wo", 4, "spread"),
          ("L1_ffn_wf", 1, "rows"), ("L1_ffn_wi", 1, "rows"), ("L1_ffn_wc", 1, "rows"),
          ("L1_ffn_wo", 1, "rows"), ("L1_ffn_uf", 1, "rows"), ("L1_ffn_ui", 1, "rows"),
          ("L1_ffn_uc", 1, "rows"), ("L1_ffn_uo", 1, "rows")]
PLAIN = [("L1_attn_w_qkv", "p n -> p n", [P, 3072]), 
         ("L0_ffn_w_gate", "p n -> p n", [P, N_EXP]), ("L0_ffn_c_fc", "e p n -> p e n", [P, N_EXP * D_FF])]
COLUMNS = ["L0_attn_ln_gamma", "L0_attn_ln_beta", "L1_xattn_bq", "L1_xattn_bk", "L1_ffn_bf",
           "L1_ffn_bi", "L1_ffn_bc", "L1_ffn_in_c"]
ROWS = ["L0_attn_b_out", "L1_attn_b_out", "L1_attn_ln_gamma", "L1_attn_ln_beta", "L1_xattn_bv",
        "L1_xattn_bo", "L1_ffn_bo"]


def setup(nc, dram, sbuf, weights, consts, x_all, ctx_all, ctxT_all, xh_all):
    with ExitStack() as ctx:
        sem = ctx.enter_context(stage_semaphores(nc, "setup"))

        raw = {}
        for name, n, _ in TURNED:
            raw[name] = ctx.enter_context(nc.sbuf_tensor(f"raw_{name}", [P, n * P], FP32))
        banks = [ctx.enter_context(nc.psum_tensor(f"turn{i}", [P, SPAN], FP32)) for i in range(8)]
        st = ctx.enter_context(nc.sbuf_tensor("st0", [P, NB, 6], FP32))
        mv = ctx.enter_context(nc.sbuf_tensor("mv0", [P, NB, 2], FP32))
        rstd = ctx.enter_context(nc.sbuf_tensor("rstd0", [P, 3, NB], FP32))
        wo_in = ctx.enter_context(nc.sbuf_tensor("wo_in", [P, P], FP32))
        wo_loaded, wo_cleared = sem("wo_loaded"), sem("wo_cleared")
        loaded = {name: sem(f"loaded_{name}") for name, _, _ in TURNED}
        count = {name: 16 for name in loaded} | {"L0_attn_w_out": 64, "L1_xattn_Wo": 1}
        x_loaded, ctx_loaded = sem("x_loaded"), sem("ctx_loaded")
        const_loaded, rest_loaded = sem("const_loaded"), sem("rest_loaded")
        turned = sem("turned")
        moved = [sem("moved_act"), sem("moved_dve")]
        stats, var_ready, bf_ready, xh_ready = sem("stats"), sem("var"), sem("bf"), sem("xh")
        pool_step = sem("pool_step")
        n_rest = len(PLAIN) + len(COLUMNS) + len(ROWS) + 17

        groups = []
        for name, n, _ in TURNED:
            for first in range(0, n, 4):
                k = min(4, n - first)
                groups.append(((loaded[name], count[name]), [raw[name][:, (first + m) * P:(first + m + 1) * P]
                                              for m in range(k)],
                               weights[name][:, first * P:(first + k) * P]))
        for first in range(0, NB, 4):
            groups.append(((ctx_loaded, 16), [ctx_all[:, (first + m) * P:(first + m + 1) * P] for m in range(4)],
                           ctxT_all[:, first * P:(first + 4) * P]))

        with nc.Block() as block:
            @block.sync
            def _(sp):
                sp.dma_start(x_all[:, :].rearrange("t (b d) -> t b d", b=NB),
                             dram["x"].rearrange("b t d -> t b d")).then_inc(x_loaded, 16)
                sp.dma_start(consts["f32"], dram["const_f32"]).then_inc(const_loaded, 16)
                for name, n, how in TURNED:
                    src = dram[name]
                    if how == "spread":
                        sp.dma_start(wo_in[:, :], src).then_inc(wo_loaded, 16)
                        continue
                    if name == "L0_attn_w_out":
                        src = src.rearrange("p (i n j d) -> p i j n d", n=4, j=2, d=64)
                        dst = raw[name][:, :].rearrange("p (i j n d) -> p i j n d", n=4, j=2, d=64)
                        for i in range(2):
                            for j in range(2):
                                sp.dma_start(dst[:, i, j], src[:, i, j]).then_inc(loaded[name], 16)
                        continue
                    if how == "rows":
                        src = src.rearrange("(n p) d -> p n d", p=P)
                    else:
                        src = src.rearrange("p (n d) -> p n d", d=P)
                    sp.dma_start(raw[name][:, :].rearrange("p (n d) -> p n d", n=n), src)\
                      .then_inc(loaded[name], 16)
                for name, s in loaded.items():
                    sp.wait_ge(s, count[name])

            @block.gpsimd
            def _(pool):
                wo = raw["L1_xattn_Wo"]
                pool.memset(wo[:, :], 0.0).then_inc(wo_cleared, 1)
                pool.wait_ge(wo_cleared, 1)
                pool.wait_ge(wo_loaded, 16)
                pool.tensor_copy(wo[:, :].rearrange("p (h d) -> p h d", d=32)[:, :, 0:8],
                                 wo_in[:, :].rearrange("p (h d) -> p h d", d=8))\
                    .then_inc(loaded["L1_xattn_Wo"], 1)
                pool.wait_ge(const_loaded, 16)
                pool.tensor_copy(consts["ident_bf"], consts["ident"]).then_inc(bf_ready, 1)
                pool.tensor_copy(consts["mask_bf"].rearrange("p (n k) -> p n k", n=4),
                                 consts["mask"].rearrange("p (o k) -> p o k", o=1)
                                 .broadcast_to([P, 4, P])).then_inc(bf_ready, 1)
                pool.wait_ge(var_ready, NB)
                link = linker(pool, pool_step)
                link(pool.tensor_scalar(rstd[:, 0, :], mv[:, :, 1], 1e-5, None, ALU.add))
                newton_rsqrt(pool, link, rstd[:, 1, :], rstd[:, 0, :], rstd[:, 2, :],
                             consts["neg_half"][:, 0:NB])

            @block.scalar
            def _(act):
                act.dma_start(ctx_all[:, :].rearrange("t (b d) -> t b d", b=NB),
                              dram["ctx_1024"].rearrange("b t d -> t b d")).then_inc(ctx_loaded, 16)
                for n in range(4):
                    for i in range(2):
                        act.dma_start(weights["L1_attn_w_out"][32 * n:32 * n + 32, i * SPAN:(i + 1) * SPAN]
                                      .rearrange("d (j m) -> d j m", m=D),
                                      dram["L1_attn_w_out"][i * SPAN + n * P:i * SPAN + (n + 1) * P, :]
                                      .rearrange("(j d) m -> d j m", j=4)).then_inc(rest_loaded, 16)
                for name, how, shape in PLAIN:
                    out = weights[name][:, :]
                    if how != "p n -> p n":
                        out = out.rearrange("p (c n) -> p c n", c=8)
                    act.dma_start(out, dram[name].rearrange(how, **({"p": P} if "(c p)" in how else {}))).then_inc(rest_loaded, 16)
                for e in range(2):
                    act.dma_start(weights["proj_last"][64 * e:64 * e + 64, :]
                                  .rearrange("p (e d) -> p e d", d=P),
                                  dram["L0_ffn_c_proj"][e::2, P:HALF, :].rearrange("e p d -> p e d"))\
                       .then_inc(rest_loaded, 16)
                for e in range(2):
                    for half in range(2):
                        act.dma_start(weights["fc_last"][:, :].rearrange("p (i h e n) -> p i h e n", h=2, e=2,
                                                                         n=64)[:, :, half, e, :],
                                      dram["L0_ffn_c_fc"][e::2, :, half * HALF + P:(half + 1) * HALF]
                                      .rearrange("i p n -> p i n")).then_inc(rest_loaded, 16)
                act.dma_start(weights["proj_first"][:, :].rearrange("p (e d) -> p e d", d=P),
                              dram["L0_ffn_c_proj"][:, 0:P, :].rearrange("e p d -> p e d"))\
                   .then_inc(rest_loaded, 16)
                for name in COLUMNS:
                    act.dma_start(weights[name], dram[name].rearrange("(p o) -> p o", o=1))\
                       .then_inc(rest_loaded, 16)
                for half in range(2):
                    name = ("L1_xattn_bq", "L1_xattn_bk")[half]
                    act.dma_start(weights[name + "_turned"],
                                  dram[name + "_turned"].rearrange("(p o) -> p o", o=1))\
                       .then_inc(rest_loaded, 16)
                for name in ROWS:
                    act.dma_start(weights[name], dram[name].rearrange("(o n) -> o n", o=1)
                                  .broadcast_to([P, P])).then_inc(rest_loaded, 16)
                for n, (_, src, dst) in enumerate(groups):
                    if n % 2 == 0:
                        act.wait_ge(turned, n + 1)
                        act.activation(dst, banks[n % 8][:, 0:len(src) * P], ACT.Copy)\
                           .then_inc(moved[0], 1)
                act.wait_ge(rest_loaded, 16 * n_rest)

            @block.tensor
            def _(pe):
                pe.wait_ge(const_loaded, 16)
                for n, ((loaded_sem, value), src, _) in enumerate(groups):
                    pe.wait_ge(loaded_sem, value)
                    if n >= 8:
                        pe.wait_ge(moved[n % 2], n // 2 - 3)
                    for m, s in enumerate(src):
                        mm = pe.transpose(banks[n % 8][:, m * P:(m + 1) * P], s, consts["ident"])
                    mm.then_inc(turned, 1)

            @block.vector
            def _(dve):
                dve.wait_ge(x_loaded, 16)
                for b in range(NB):
                    dve.bn_stats(st[:, b, :], x_all[:, b * D:(b + 1) * D]).then_inc(stats, 1)
                for b in range(NB):
                    dve.wait_ge(stats, b + 1)
                    dve.bn_aggr(mv[:, b, :], st[:, b, :]).then_inc(var_ready, 1)
                for n, (_, src, dst) in enumerate(groups):
                    if n % 2 == 1:
                        dve.wait_ge(turned, n + 1)
                        dve.tensor_copy(dst, banks[n % 8][:, 0:len(src) * P]).then_inc(moved[1], 1)
                dve.wait_ge(pool_step, 6)
                dve.wait_ge(var_ready, NB)
                for b in range(NB):
                    dve.tensor_scalar(xh_all[:, b * D:(b + 1) * D], x_all[:, b * D:(b + 1) * D],
                                      mv[:, b, 0:1], rstd[:, 1, b:b + 1], ALU.subtract, ALU.mult)\
                       .then_inc(xh_ready, 1)


CONST_COLS = {"ident": P, "before": P, "ones": P, "cos": P, "sin": P, "cos_q": P, "sin_q": P,
              "mask": P, "iota8": 8, "block_of": 4, "neg_half": NB}


def decoder(nc, dram, out, stages):
    with ExitStack() as ctx:
        def sb(name, shape, dt=FP32):
            return ctx.enter_context(nc.sbuf_tensor(name, shape, dt))

        x_all = sb("x_all", [P, NB * D])
        ctx_all = sb("ctx_all", [P, NB * D])
        ctxT_all = sb("ctxT_all", [P, NB * P])
        f32 = sb("const_f32_sb", [P, sum(CONST_COLS.values())])
        bf = sb("const_bf16_sb", [P, P + SPAN], BF16)
        consts = {"f32": f32[:, :], "ident_bf": bf[:, 0:P], "mask_bf": bf[:, P:]}
        at = 0
        for name, n in CONST_COLS.items():
            consts[name] = f32[:, at:at + n]
            at += n
        weights = {name: sb(f"w_{name}", [P, n * P]) for name, n, _ in TURNED}
        weights |= {name: sb(f"w_{name}", shape) for name, _, shape in PLAIN}
        weights["L1_attn_w_out"] = sb("w_L1_attn_w_out", [P, 8 * D])
        weights["proj_first"] = sb("proj_first", [P, N_EXP * D])
        weights["fc_last"] = sb("fc_last", [P, N_EXP * P])
        weights["proj_last"] = sb("proj_last", [P, N_EXP // 2 * D])
        cols = sb("columns", [P, len(COLUMNS) + 2])
        for n, name in enumerate(COLUMNS + ["L1_xattn_bq_turned", "L1_xattn_bk_turned"]):
            weights[name] = cols[:, n:n + 1]
        rows = sb("rows", [P, len(ROWS) * P])
        for n, name in enumerate(ROWS):
            weights[name] = rows[:, n * P:(n + 1) * P]
        out_done = ctx.enter_context(nc.semaphore("out_done"))

        with nc.sbuf_tensor("xh_all", [P, NB * D], FP32) as xh_all:
            setup(nc, dram, sb, weights, consts, x_all, ctx_all, ctxT_all, xh_all)
            if "A" in stages:
                attention_stage(nc, "causal", x_all, xh_all, consts,
                                {"wqkv": weights["L0_attn_w_qkv"], "wo": weights["L0_attn_w_out"],
                                 "bout": weights["L0_attn_b_out"],
                                 "gamma_col": weights["L0_attn_ln_gamma"],
                                 "beta_col": weights["L0_attn_ln_beta"]})
        if "B" in stages:
            alignment_stage(nc, consts, x_all, ctx_all, ctxT_all)
        if "C" in stages:
            experts_stage(nc, consts, weights, x_all)
        if "D" in stages:
            attention_stage(nc, "plain", x_all, x_all, consts,
                            {"wqkv": weights["L1_attn_w_qkv"], "wo": weights["L1_attn_w_out"],
                             "bout": weights["L1_attn_b_out"], "gamma": weights["L1_attn_ln_gamma"],
                             "beta": weights["L1_attn_ln_beta"]})
        if "E" in stages:
            with ExitStack() as part:
                kT_all = part.enter_context(nc.sbuf_tensor("kT_all", [P, NB * P], FP32))
                v_all = part.enter_context(nc.sbuf_tensor("v_all", [P, NB * D], FP32))
                turned = part.enter_context(nc.sbuf_tensor("w_turned", [P, 2 * P], FP32))
                context_keys(nc, consts, weights, ctxT_all, [turned[:, 0:P], turned[:, P:2 * P]],
                             kT_all, v_all)
                attention_stage(nc, "rope", x_all, x_all, consts | {"kT_all": kT_all, "v_all": v_all},
                                {"wq": weights["L1_xattn_Wq"][:, :], "wq_turned": turned[:, P:2 * P],
                                 "bq": weights["L1_xattn_bq"], "bq_turned": weights["L1_xattn_bq_turned"],
                                 "wo": weights["L1_xattn_Wo"][:, :], "bout": weights["L1_xattn_bo"]})
        if "F" in stages:
            with nc.sbuf_tensor("rnn_xT", [P, NB * P], FP32) as xT:
                turn_all(nc, "rnn", consts, x_all, xT)
                recurrent_stage(nc, consts, weights, x_all, xT)
        with nc.Block() as block:
            @block.sync
            def _(sp):
                sp.dma_start(out.rearrange("b t d -> t b d"),
                             x_all[:, :].rearrange("t (b d) -> t b d", b=NB)).then_inc(out_done, 16)
                sp.wait_ge(out_done, 16)


def constants():
    f = np.float32
    d = np.arange(P)
    inv = (1.0 / 10000.0 ** (np.arange(0, 8, 2, dtype=f) / f(8))).astype(f)
    angle = (np.arange(P, dtype=f)[None, :] * inv[d % 4][:, None]).astype(f)
    cos, sin = np.cos(angle.astype(np.float64)), np.sin(angle.astype(np.float64))
    sin = np.where((d % 8 < 4)[:, None], -sin, sin)
    parts = {"ident": np.eye(P), "before": np.triu(np.ones((P, P)), 1), "ones": np.ones((P, P)),
             "cos": cos, "sin": sin, "cos_q": cos * 8 ** -0.5, "sin_q": sin * 8 ** -0.5,
             "iota8": np.tile(np.arange(8), (P, 1)),
             "block_of": (d[:, None] // 8 % 4 == np.arange(4)[None, :]) * 1.0,
             "mask": np.where(d[None, :] > d[:, None], -BIG, 0.0),
             "neg_half": np.full((P, NB), -0.5)}
    f32 = np.concatenate([parts[n].astype(f) for n in CONST_COLS], axis=1)
    return f32


_OUTS = [((NB, P, D), "float32")]


def kernel(**inputs):
    import concourse.bacc as _bacc
    from concourse import mybir as _mybir
    from concourse.bass_utils import run_bass_kernel_spmd as _run

    nc = _bacc.Bacc("TRN2", target_bir_lowering=False, num_devices=1)
    arrays = {n: np.ascontiguousarray(a) for n, a in inputs.items()}
    arrays["const_f32"] = constants()
    for n in ("L1_xattn_bq", "L1_xattn_bk"):
        arrays[n + "_turned"] = np.ascontiguousarray(
            arrays[n].reshape(16, 2, 4)[:, ::-1, :].reshape(P))
    dram, given = {}, {}
    for n, a in arrays.items():
        given[f"in_{n}_dram"] = a
        dram[n] = nc.dram_tensor(f"in_{n}_dram", a.shape, _mybir.dt.from_np(a.dtype),
                                 kind="ExternalInput").ap()
    out = nc.dram_tensor("out_0_dram", _OUTS[0][0], _mybir.dt.float32, kind="ExternalOutput").ap()
    decoder(nc, dram, out, STAGES)
    r = _run(nc, [given], core_ids=[0])
    return r.results[0]["out_0_dram"]


STAGES = "ABCDEF"
```

```python
import math
from contextlib import ExitStack, contextmanager

import numpy as np
import concourse.bass as bass
from concourse import mybir

FP32 = mybir.dt.float32
BF16 = mybir.dt.bfloat16
FP32R = mybir.dt.float32r
ALU = mybir.AluOpType
ACT = mybir.ActivationFunctionType
AX = mybir.AxisListType

P = 128
NB = 16
D = 128
SPAN = 512
BIG = 1e30
N_EXP = 8
CAPACITY = 512
D_FF = 384
HALF = D_FF // 2


@contextmanager
def stage_semaphores(nc, stage):
    taken = []

    def sem(name):
        taken.append(nc.alloc_semaphore(name=f"{stage}_{name}"))
        return taken[-1]
    yield sem
    nc.clear_and_free_semaphores(taken)
    nc.all_engine_barrier()


def wait(eng, sem, value):
    if isinstance(value, int) and value <= 0:
        return
    eng.wait_ge(sem, value)


def exists(b):
    return not isinstance(b, int) or 0 <= b < NB


def spread(ap, shape):
    return ap.rearrange("p (n o) -> p n o", o=1).broadcast_to(shape)


def newton_rsqrt(pool, chain, y, v, t, halves):
    chain(pool.tensor_tensor(y, v, halves, op=ALU.pow))
    chain(pool.tensor_tensor(t, y, y, op=ALU.mult))
    chain(pool.tensor_tensor(t, t, v, op=ALU.mult))
    chain(pool.tensor_scalar(t, t, -0.5, 1.5, ALU.mult, ALU.add))
    chain(pool.tensor_tensor(y, y, t, op=ALU.mult))


def wait_alone(eng, sem, value, spare):
    if isinstance(value, int):
        wait(eng, sem, value)
        return
    register, started = spare
    eng.reg_mov(register, value)
    eng.wait_ge(started, 1)
    eng.wait_ge(sem, register)


def linker(eng, sem, base=0, spare=None):
    count = [0]

    def link(ins):
        count[0] += 1
        ins.then_inc(sem, 1)
        wait_alone(eng, sem, base + count[0], spare)
    return link


def attention_stage(nc, kind, x_all, xin_all, consts, weights, meanwhile=None):
    rope = kind == "rope"
    heads = {"causal": 16, "plain": 32, "rope": 16}[kind]
    dh = {"causal": 64, "plain": 32, "rope": 8}[kind]
    G = heads // 4
    rows = 128 // (4 if rope else 1)
    dv = 32 if rope else dh
    inner = heads * dv
    per_chunk = P // dv
    chunks = 4 // per_chunk
    fills = SPAN // P // chunks
    o_banks = G // fills
    last_post = 2 if kind == "plain" else 1

    if rope:
        ITEMS = [("q0", 1, 1), ("y", 2, -1), ("xt", 3, 2)]
    elif G == 4:
        ITEMS = [("q0", 0, 1), ("k0", 0, 1), ("v0", 1, 1), ("q1", 1, 1), ("y", 2, -1),
                 ("k1", 3, 1), ("v1", 3, 1), ("xt", 3, 2)]
    else:
        ITEMS = [("q0", 0, 1), ("k0", 1, 1), ("y", 2, -1), ("v0", 4, 1),
                 ("q1", 5, 1), ("k1", 6, 1), ("v1", 7, 1), ("xt", 7, 2)]
    y_end = 3 if kind == "plain" else 2
    names = [k for k, _, _ in ITEMS]
    PROBT_ON_VECTOR = {"causal": (), "plain": (), "rope": ()}[kind]
    ON_VECTOR = {"causal": ("y", "xt"), "plain": ("y",), "rope": ("y", "q0")}[kind]

    def heads_of(g):
        if rope:
            return [(32 * g, 0, 4 * g + n) for n in range(4)]
        per = 128 // dh
        return [(dh * (g % per), 4 * (g // per) + n, (4 * (g // per) + n) * per + g % per)
                for n in range(4)]

    with ExitStack() as ctx:
        def sb(name, shape, dt=FP32):
            return ctx.enter_context(nc.sbuf_tensor(f"{kind}_{name}", shape, dt))

        def pb(name):
            return ctx.enter_context(nc.psum_tensor(f"{kind}_{name}", [P, SPAN], FP32))

        sem = ctx.enter_context(stage_semaphores(nc, kind))

        def pair(name, shape):
            return [sb(f"{name}{i}", shape) for i in range(2)]

        xin = pair("xin", [P, D])
        xT = pair("xT", [P, P])
        if rope:
            qT = pair("qT", [P, P])
            qr = pair("qr", [P, 2, P])
            kT = pair("kT", [P, 4, P])
        else:
            qT = pair("qT", [P, inner])
            kT = pair("kT", [P, inner])
            x_lead = [sb(f"x_lead{i}", [P, P], FP32R) for i in range(2)]
            x_left = [sb(f"x_left{i}", [P, P], FP32R) for i in range(2)]
        v = pair("v", [P, heads, dv])
        prob = pair("prob", [P, SPAN])
        probT = pair("probT", [P, SPAN])
        negmax = sb("negmax", [P, 4, 4])
        total = sb("total", [P, 4, 4])
        share = sb("share", [P, 4, 4])
        oT = sb("oT", [P, inner])
        xres = pair("xres", [P, D])
        z = pair("z", [P, D])
        z2 = pair("z2", [P, D])
        zt = sb("zt", [P, D])
        st = sb("st", [P, 2, 6])
        mv = sb("mv", [P, 2, 2])
        mv2 = sb("mv2", [P, 2, 2])
        rs = sb("rs", [P, 1])
        rv = sb("rv", [P, 1])
        rt = sb("rt", [P, 1])

        pmm = [pb("pmm0"), pb("pmm1")]
        psc = [pb("psc0"), pb("psc1")]
        ppt = [pb("ppt0"), pb("ppt1")]
        po = [pb("po0"), pb("po1")]

        made = {k: sem(f"made_{k}") for k in names}
        moved = {k: sem(f"moved_{k}") for k in names}
        xin_ready = sem("xin_ready")
        kv_ready = sem("kv_ready")
        zeros_ready = sem("zeros_ready")
        scores_made = sem("scores_made")
        max_ready = sem("max_ready")
        prob_ready = sem("prob_ready")
        prob_turned = sem("prob_turned")
        probT_ready = [sem("probT_ready0"), sem("probT_ready1")]
        pv_made = sem("pv_made")
        share_ready = sem("share_ready")
        norm_ready = sem("norm_ready")
        o_moved = sem("o_moved")
        xres_ready = sem("xres_ready")
        z_ready = sem("z_ready")
        zst_ready = sem("zst_ready")
        stats_ready = sem("stats_ready")
        z2_ready = sem("z2_ready")
        z2st_ready = sem("z2st_ready")
        stats2_ready = sem("stats2_ready")
        qr_ready = sem("qr_ready")
        parts_ready = sem("parts_ready")
        done = sem("done")
        pool_step = sem("pool_step")
        pool_step2 = sem("pool_step2")
        dve_started = sem("dve_started")
        pool_started = sem("pool_started")

        def bank_free(eng, b, n):
            at = n
            bb = b
            for _ in range(5 * len(ITEMS)):
                at -= 1
                if at < 0:
                    at += len(ITEMS)
                    bb = bb - 1
                k, _, off = ITEMS[at]
                if at % 2 == n % 2 and exists(bb + off):
                    wait(eng, moved[k], bb + off + 1)
                    return

        def bodies(eng, body):
            for b in range(-2, 2):
                body(b, b % 2)
            with eng.Fori(1, NB // 2 - 1) as i:
                for u in range(2):
                    body(i * 2 + u, u)
            for b in range(NB - 2, NB + last_post):
                body(b, b % 2)

        with nc.Block() as block:
            if meanwhile:
                @block.sync
                def _(sp):
                    meanwhile(sp)

            @block.tensor
            def _(pe):
                def scores(b, g, p, t):
                    if g == 0:
                        wait(pe, moved["q0"], b + 1)
                        wait(pe, kv_ready if rope else moved["k0"], b + 1)
                    elif g == G // 2 and not rope:
                        wait(pe, moved["q1"], b + 1)
                        wait(pe, moved["k1"], b + 1)
                    wait(pe, prob_ready, t - 1)
                    s = psc[g % 2]
                    if rope:
                        r = 32 * g
                        pe.matmul(s[:, :], qT[p][r:r + rows, :], kT[p][r:r + rows, :, :],
                                  start=True, stop=True).then_inc(scores_made, 1)
                        return
                    causal = kind == "causal"
                    if causal:
                        pe.matmul(s[:, :], consts["ident_bf"], consts["mask_bf"], start=True,
                                  stop=False, skip_group_check=True)
                    for n, (r, c, h) in enumerate(heads_of(g)):
                        mm = pe.matmul(s[:, n * P:(n + 1) * P], qT[p][r:r + dh, c * P:(c + 1) * P],
                                       kT[p][r:r + dh, c * P:(c + 1) * P], start=not causal,
                                       stop=True, skip_group_check=causal)
                    mm.then_inc(scores_made, 1)

                def output_product(m, first, end):
                    for c in range(first, end):
                        mm = pe.matmul(m[:, 0:P], oT[:, c * P:(c + 1) * P],
                                       weights["wo"][:, c * P:(c + 1) * P],
                                       start=c == 0, stop=c == inner // P - 1)
                    return mm

                def item(k, b, p, bank):
                    m = pmm[bank]
                    if k == "xt":
                        wait(pe, xin_ready, b + 1)
                        mm = pe.transpose(m[:, 0:P], xin[p][:, :], consts["ident"])
                    elif k == "q0" and rope:
                        wait(pe, moved["xt"], b + 1)
                        pe.matmul(m[:, 0:P], weights["wq"], xT[p][:, :], start=True, stop=True)
                        mm = pe.matmul(m[:, P:2 * P], weights["wq_turned"], xT[p][:, :],
                                       start=True, stop=True)
                    elif k[0] in "qk":
                        wait(pe, moved["xt"], b + 1)
                        first = (0 if k[0] == "q" else inner) + int(k[1]) * SPAN
                        for n in range(4):
                            mm = pe.matmul(m[:, n * P:(n + 1) * P],
                                           weights["wqkv"][:, first + n * P:first + (n + 1) * P],
                                           xT[p][:, :], start=True, stop=True)
                    elif k[0] == "v":
                        cols = slice(int(k[1]) * SPAN, (int(k[1]) + 1) * SPAN)
                        wait(pe, parts_ready, 2 * b + 2)
                        pe.matmul(m[:, :], x_lead[p][:, :], weights["wv_lead"][:, cols], start=True, stop=False)
                        pe.matmul(m[:, :], x_lead[p][:, :], weights["wv_left"][:, cols], start=False, stop=False)
                        mm = pe.matmul(m[:, :], x_left[p][:, :], weights["wv_lead"][:, cols],
                                       start=False, stop=True)
                    else:
                        wait(pe, o_moved, (b + 1) * o_banks)
                        mm = output_product(m, 0, inner // P // (1 if y_end == 2 else 2))
                        if y_end != 2:
                            return
                    mm.then_inc(made[k], 1)

                def body(b, p):
                    for g in range(G):
                        t = b * G + g
                        bs = b + (g + 2) // G
                        if exists(bs):
                            scores(bs, (g + 2) % G, (p + (g + 2) // G) % 2, t + 2)
                        for n, (k, slot, off) in enumerate(ITEMS):
                            if slot == g and exists(b + off):
                                bank_free(pe, b, n)
                                item(k, b + off, (p + off) % 2, n % 2)
                        if g == 3 and y_end == 3 and exists(b - 1):
                            output_product(pmm[names.index("y") % 2], inner // P // 2, inner // P)\
                                .then_inc(made["y"], 1)
                        if exists(b):
                            wait(pe, norm_ready, t + 1)
                            wait(pe, probT_ready[g % 2], b * (G // 2) + g // 2)
                            for n in range(4):
                                mm = pe.transpose(ppt[g % 2][:, n * P:(n + 1) * P],
                                                  prob[g % 2][:, n * P:(n + 1) * P],
                                                  consts["ident"])
                            mm.then_inc(prob_turned, 1)
                        bv = b - (g == 0)
                        if exists(bv):
                            gv, pv = (g - 1) % G, (p + (g == 0)) % 2
                            if rope and gv == 0:
                                wait(pe, kv_ready, bv + 1)
                                wait(pe, zeros_ready, 2)
                            elif gv == 0:
                                wait(pe, moved["v0"], bv + 1)
                            elif gv == G // 2 and not rope:
                                wait(pe, moved["v1"], bv + 1)
                            wait(pe, probT_ready[gv % 2], bv * (G // 2) + gv // 2 + 1)
                            if gv % fills == 0:
                                wait(pe, o_moved, (bv - 1) * 2 + gv // fills + 1 if o_banks == 2 else bv - 1)
                            bank = po[gv // fills if o_banks == 2 else pv]
                            for n, (_, _, h) in enumerate(heads_of(gv)):
                                r = n % per_chunk * dv
                                c = gv % fills * chunks + n // per_chunk
                                mm = pe.matmul(bank[r:r + dv, c * P:(c + 1) * P], v[pv][:, h, :],
                                               probT[gv % 2][:, n * P:(n + 1) * P], start=True, stop=True)
                            mm.then_inc(pv_made, 1)

                bodies(pe, body)
                if kind == "plain":
                    pe.wait_ge(prob_ready, NB * G)
                    for _ in range(8):
                        pe.matmul(psc[0][:, :], consts["ident"], consts["f32"][:, 0:SPAN], start=True, stop=True)

            def move_item(eng, k, b, p, bank):
                m = pmm[bank]
                on_act = k not in ON_VECTOR
                wait(eng, made[k], b + 1)

                def copy(out, in_, scale=1.0):
                    if on_act:
                        return eng.activation(out, in_, ACT.Copy, scale=scale)
                    if scale == 1.0:
                        return eng.tensor_copy(out, in_)
                    return eng.tensor_scalar(out, in_, scale, None, ALU.mult)

                if k == "xt":
                    if not rope:
                        wait(eng, parts_ready, 2 * b - 2)
                    if kind == "causal":
                        ins = eng.tensor_scalar(xT[p][:, :], m[:, 0:P], weights["gamma_col"],
                                                weights["beta_col"], ALU.mult, ALU.add)
                    else:
                        ins = copy(xT[p][:, :], m[:, 0:P])
                elif k[0] == "q":
                    ins = copy(qT[p][:, int(k[1]) * SPAN:(int(k[1]) + 1) * SPAN], m[:, :], dh ** -0.5)
                elif k[0] == "k":
                    ins = copy(kT[p][:, int(k[1]) * SPAN:(int(k[1]) + 1) * SPAN], m[:, :])
                elif k[0] == "v":
                    nh = SPAN // dh
                    ins = copy(v[p][:, int(k[1]) * nh:(int(k[1]) + 1) * nh, 0:dh],
                               m[:, :].rearrange("p (h d) -> p h d", d=dh))
                ins.then_inc(moved[k], 1)

            @block.scalar
            def _(act):
                act.preload_act_table(ACT.Exp)

                def body(b, p):
                    for g in range(G):
                        t = b * G + g
                        be, ge = b + (g + 1) // G, (g + 1) % G
                        if exists(be):
                            wait(act, max_ready, t + 2)
                            wait(act, prob_turned, t)
                            for n in range(4):
                                ins = act.activation(prob[ge % 2][:, n * P:(n + 1) * P],
                                                     psc[ge % 2][:, n * P:(n + 1) * P], ACT.Exp,
                                                     bias=negmax[:, ge % 4, n:n + 1],
                                                     accum_out=total[:, ge % 4, n:n + 1])
                            ins.then_inc(prob_ready, 1)
                        for n, (k, slot, off) in enumerate(ITEMS):
                            if slot == g and exists(b + off) and k not in ON_VECTOR:
                                move_item(act, k, b + off, (p + off) % 2, n % 2)
                        if exists(b) and g % 2 not in PROBT_ON_VECTOR:
                            wait(act, prob_turned, t + 1)
                            wait(act, pv_made, t - 1)
                            act.activation(probT[g % 2][:, :], ppt[g % 2][:, :], ACT.Copy)\
                               .then_inc(probT_ready[g % 2], 1)

                bodies(act, body)

            @block.vector
            def _(dve):
                dve_spare = (dve.alloc_register("spare_dve_" + kind), dve_started)
                dve.engine_nop().then_inc(dve_started, 1)
                def body(b, p):
                    for g in range(G):
                        t = b * G + g
                        if exists(b):
                            wait(dve, prob_ready, t + 1)
                            dve.reciprocal(share[:, g % 4, :], total[:, g % 4, :]).then_inc(share_ready, 1)
                            wait(dve, share_ready, t + 1)
                            pr = prob[g % 2][:, :].rearrange("p (h k) -> p h k", h=4)
                            dve.tensor_tensor(pr, pr, spread(share[:, g % 4, :], [P, 4, P]), op=ALU.mult)\
                               .then_inc(norm_ready, 1)
                        bm = b + (g + 2) // G
                        if exists(bm):
                            gm = (g + 2) % G
                            wait(dve, scores_made, t + 3)
                            wait(dve, prob_ready, t - 1)
                            dve.tensor_reduce(negmax[:, gm % 4, :],
                                              psc[gm % 2][:, :].rearrange("p (h k) -> p h k", h=4),
                                              AX.X, ALU.max, negate=True).then_inc(max_ready, 1)
                        if exists(b) and g % 2 in PROBT_ON_VECTOR:
                            wait(dve, prob_turned, t + 1)
                            wait(dve, pv_made, t - 1)
                            dve.tensor_copy(probT[g % 2][:, :], ppt[g % 2][:, :])\
                               .then_inc(probT_ready[g % 2], 1)
                        for n, (k, slot, off) in enumerate(ITEMS):
                            if (y_end if k == "y" else slot) != g or not exists(b + off) or k not in ON_VECTOR:
                                continue
                            bi, pi, m = b + off, (p + off) % 2, pmm[n % 2]
                            if k == "y":
                                wait(dve, made[k], bi + 1)
                                wait(dve, xres_ready, bi + 1)
                                dve.tensor_tensor(z[pi][:, :], m[:, 0:P],
                                                  weights["bout"] if kind == "plain" else xres[pi][:, :],
                                                  op=ALU.add).then_inc(moved[k], 1)
                            elif k == "q0" and rope:
                                wait(dve, made[k], bi + 1)
                                dve.scalar_tensor_tensor(qr[pi][:, 0, :], m[:, 0:P], weights["bq"],
                                                         consts["cos_q"], ALU.add, ALU.mult)\
                                   .then_inc(qr_ready, 1)
                                dve.scalar_tensor_tensor(qr[pi][:, 1, :], m[:, P:2 * P],
                                                         weights["bq_turned"], consts["sin_q"],
                                                         ALU.add, ALU.mult).then_inc(qr_ready, 1)
                                wait(dve, qr_ready, 2 * bi + 2)
                                dve.tensor_tensor(qT[pi][:, :], qr[pi][:, 0, :], qr[pi][:, 1, :],
                                                  op=ALU.add).then_inc(moved[k], 1)
                            else:
                                move_item(dve, k, bi, pi, n % 2)
                        for half, at, back in ((0, fills + 1, 0), (1, 1, 1)) if o_banks == 2 else ((0, 1, 1),):
                            if g == at and exists(b - back):
                                bo = b - back
                                wait(dve, pv_made, bo * G + (half + 1) * fills)
                                wait(dve, made["y"], bo)
                                dve.tensor_copy(oT[:, half * SPAN:(half + 1) * SPAN],
                                                po[half if o_banks == 2 else (p + back) % 2][:, :])\
                                   .then_inc(o_moved, 1)
                        if g == y_end and exists(b - 1):
                            wait(dve, moved["y"], b)
                            dve.bn_stats(st[:, 0, :], z[1 - p][:, :]).then_inc(zst_ready, 1)
                            wait_alone(dve, zst_ready, b, dve_spare)
                            dve.bn_aggr(mv[:, 1 - p, :], st[:, 0, :]).then_inc(stats_ready, 1)
                        if kind == "plain" and g == 1 and exists(b - 2):
                            wait(dve, z2_ready, b - 1)
                            dve.bn_stats(st[:, 1, :], z2[p][:, :]).then_inc(z2st_ready, 1)
                            wait_alone(dve, z2st_ready, b - 1, dve_spare)
                            dve.bn_aggr(mv2[:, p, :], st[:, 1, :]).then_inc(stats2_ready, 1)

                bodies(dve, body)

            @block.gpsimd
            def _(pool):
                pool_spare = (pool.alloc_register("spare_pool_" + kind), pool_started)
                pool.engine_nop().then_inc(pool_started, 1)
                if rope:
                    for i in range(2):
                        pool.memset(v[i][:, :, dh:dv], 0.0).then_inc(zeros_ready, 1)

                def normalise(b, p, stats, zz, out, eps, link, last):
                    link(pool.tensor_scalar(rv[:, :], stats[:, p, 1:2], eps, None, ALU.add))
                    newton_rsqrt(pool, link, rs[:, :], rv[:, :], rt[:, :], consts["neg_half"][:, 0:1])
                    link(pool.tensor_scalar(zt[:, :], zz[p][:, :], stats[:, p, 0:1], None, ALU.subtract))
                    ins = pool.tensor_tensor(out, zt[:, :], rs[:, 0:1].broadcast_to([P, D]), op=ALU.mult)
                    if last:
                        ins.then_inc(last, 1)
                        wait_alone(pool, last, b + 1, pool_spare)
                    else:
                        link(ins)

                def body(b, p):
                    if exists(b + 2):
                        wait_alone(pool, made["xt"], b + 1, pool_spare)
                        pool.tensor_copy(xin[p][:, :], xin_all[:, bass.ds((b + 2) * D, D)])\
                            .then_inc(xin_ready, 1)
                    if not rope and exists(b + 1):
                        q = (p + 1) % 2
                        wait_alone(pool, made["v1"], b, pool_spare)
                        wait_alone(pool, moved["xt"], b + 2, pool_spare)
                        pool.tensor_copy(x_lead[q][:, :], xT[q][:, :]).then_inc(parts_ready, 1)
                        wait_alone(pool, parts_ready, 2 * b + 3, pool_spare)
                        pool.tensor_tensor(x_left[q][:, :], xT[q][:, :], x_lead[q][:, :].bitcast(FP32),
                                           op=ALU.subtract).then_inc(parts_ready, 1)
                    if rope and exists(b + 1):
                        q = (p + 1) % 2
                        wait_alone(pool, pv_made, b * G, pool_spare)
                        pool.tensor_tensor(kT[q][:, :, :],
                                           consts["kT_all"][:, bass.ds((b + 1) * P, P)]
                                           .rearrange("p (o k) -> p o k", o=1).broadcast_to([P, 4, P]),
                                           spread(consts["block_of"], [P, 4, P]), op=ALU.mult)
                        pool.tensor_copy(v[q][:, :, 0:dh],
                                         consts["v_all"][:, bass.ds((b + 1) * P, P)]
                                         .rearrange("p (h d) -> p h d", d=dh)).then_inc(kv_ready, 1)
                    if exists(b) and kind != "plain":
                        wait_alone(pool, moved["y"], b - 1, pool_spare)
                        pool.tensor_tensor(xres[p][:, :], x_all[:, bass.ds(b * D, D)], weights["bout"],
                                           op=ALU.add).then_inc(xres_ready, 1)
                    elif exists(b):
                        pool.tensor_copy(xres[p][:, :], x_all[:, bass.ds(b * D, D)])\
                            .then_inc(xres_ready, 1)
                    if kind == "plain" and exists(b - 2):
                        wait_alone(pool, stats2_ready, b - 1, pool_spare)
                        normalise(b - 2, p, mv2, z2, x_all[:, bass.ds((b - 2) * D, D)], 1e-5,
                                  linker(pool, pool_step2, (b - 2) * 7, pool_spare), done)
                    if exists(b - 1):
                        q = (p + 1) % 2
                        wait_alone(pool, stats_ready, b, pool_spare)
                        if kind == "plain":
                            link = linker(pool, pool_step, (b - 1) * 10, pool_spare)
                            normalise(b - 1, q, mv, z, zt[:, :], 1e-6, link, None)
                            link(pool.tensor_tensor(zt[:, :], zt[:, :], weights["gamma"], op=ALU.mult))
                            link(pool.tensor_tensor(zt[:, :], zt[:, :], weights["beta"], op=ALU.add))
                            pool.tensor_tensor(z2[q][:, :], zt[:, :], xres[q][:, :], op=ALU.add)\
                                .then_inc(z2_ready, 1)
                            wait_alone(pool, z2_ready, b, pool_spare)
                        else:
                            normalise(b - 1, q, mv, z, x_all[:, bass.ds((b - 1) * D, D)], 1e-5,
                                      linker(pool, pool_step, (b - 1) * 7, pool_spare), done)

                bodies(pool, body)


def layer_norm_all(nc, name, consts, z, x_all):
    with ExitStack() as ctx:
        def sem(n):
            return ctx.enter_context(nc.semaphore(f"{name}_ln_{n}"))

        st = ctx.enter_context(nc.sbuf_tensor(f"{name}_st", [P, NB, 6], FP32))
        mv = ctx.enter_context(nc.sbuf_tensor(f"{name}_mv", [P, NB, 2], FP32))
        var = ctx.enter_context(nc.sbuf_tensor(f"{name}_var", [P, NB], FP32))
        rough = ctx.enter_context(nc.sbuf_tensor(f"{name}_rough", [P, NB], FP32))
        fix = ctx.enter_context(nc.sbuf_tensor(f"{name}_fix", [P, NB], FP32))
        scale = ctx.enter_context(nc.sbuf_tensor(f"{name}_scale", [P, NB], FP32))
        shift = ctx.enter_context(nc.sbuf_tensor(f"{name}_shift", [P, NB], FP32))
        stats, variances, step, applied = sem("stats"), sem("variances"), sem("step"), sem("applied")
        rough_ready = sem("rough_ready")
        with nc.Block() as block:
            @block.vector
            def _(dve):
                link = linker(dve, step)
                for b in range(NB):
                    dve.bn_stats(st[:, b, :], z[:, b * D:(b + 1) * D]).then_inc(stats, 1)
                for b in range(NB):
                    dve.wait_ge(stats, b + 1)
                    dve.bn_aggr(mv[:, b, :], st[:, b, :]).then_inc(variances, 1)
                dve.wait_ge(variances, NB)
                link(dve.tensor_scalar(var[:, :], mv[:, :, 1], 1e-5, None, ALU.add))
                dve.wait_ge(rough_ready, 1)
                link(dve.tensor_tensor(fix[:, :], rough[:, :], rough[:, :], op=ALU.mult))
                link(dve.tensor_tensor(fix[:, :], fix[:, :], var[:, :], op=ALU.mult))
                link(dve.tensor_scalar(fix[:, :], fix[:, :], -0.5, 1.5, ALU.mult, ALU.add))
                link(dve.tensor_tensor(scale[:, :], rough[:, :], fix[:, :], op=ALU.mult))
                dve.scalar_tensor_tensor(shift[:, :], mv[:, :, 0], -1.0, scale[:, :], ALU.mult, ALU.mult)\
                   .then_inc(step, 1)
                for b in range(0, NB, 2):
                    dve.tensor_scalar(x_all[:, b * D:(b + 1) * D], z[:, b * D:(b + 1) * D],
                                      mv[:, b, 0:1], scale[:, b:b + 1], ALU.subtract, ALU.mult)\
                       .then_inc(applied, 1)

            @block.scalar
            def _(act):
                act.preload_act_table(ACT.Abs_reciprocal_sqrt)
                act.wait_ge(step, 1)
                act.activation(rough[:, :], var[:, :], ACT.Abs_reciprocal_sqrt).then_inc(rough_ready, 1)
                act.wait_ge(step, 6)
                for b in range(1, NB, 2):
                    act.activation(x_all[:, b * D:(b + 1) * D], z[:, b * D:(b + 1) * D], ACT.Identity,
                                   bias=shift[:, b:b + 1], scale=scale[:, b:b + 1]).then_inc(applied, 1)


def alignment_stage(nc, consts, x_all, ctx_all, ctxT_all, later_loads, later_work):
    R1 = P + 1
    BLOCKS = [(0, 8), (8, 40), (40, 72), (72, 104), (104, 120), (120, 128)]
    ctx = ExitStack()
    with ctx:
        sem = ctx.enter_context(stage_semaphores(nc, "dtw"))

        def sb(name, shape, where=ctx):
            return where.enter_context(nc.sbuf_tensor(f"dtw_{name}", shape, FP32))

        dist_dram = nc.dram_tensor("dist_dram", [NB, P, P], FP32, kind="Internal").ap()
        cost_dram = nc.dram_tensor("cost_dram", [NB, R1, R1], FP32, kind="Internal").ap()
        jump_dram = nc.dram_tensor("jump_dram", [NB, P, P], FP32, kind="Internal").ap()

        with ExitStack() as part:
            xsq = sb("xsq", [P, NB * P], part)
            xm2 = sb("xm2", [P, NB * P], part)
            csq = sb("csq", [P, NB * D], part)
            norm = sb("norm", [P, NB], part)
            a = sb("a", [P, NB * P], part)
            s = sb("s", [P, NB * P], part)
            sq = sb("sq", [P, NB * P], part)
            inv = sb("inv", [P, NB * P], part)
            turn = [part.enter_context(nc.psum_tensor(f"dtw_turn{i}", [P, SPAN], FP32)) for i in range(4)]
            dist = [part.enter_context(nc.psum_tensor(f"dtw_dist{i}", [P, SPAN], FP32)) for i in range(4)]
            turned, squared, doubled, norms = sem("turned"), sem("squared"), sem("doubled"), sem("norms")
            norm_step = sem("norm_step")
            dist_made, a_ready, s_ready = sem("dist_made"), sem("a_ready"), sem("s_ready")
            sq_ready, r_ready, inv_ready = sem("sq"), sem("r"), sem("inv")
            fix_ready, d_ready, d_stored = sem("fix"), sem("d"), sem("d_stored")

            def chunk(t, c):
                return t[:, c * SPAN:(c + 1) * SPAN]

            with nc.Block() as block:
                @block.tensor
                def _(pe):
                    for c in range(4):
                        for m in range(4):
                            b = 4 * c + m
                            mm = pe.transpose(turn[c][:, m * P:(m + 1) * P], x_all[:, b * D:(b + 1) * D],
                                              consts["ident"])
                        mm.then_inc(turned, 1)
                    for c in range(4):
                        pe.wait_ge(squared, c + 1)
                        pe.matmul(dist[c][:, :], consts["ones"], chunk(xsq, c), start=True,
                                  stop=False, skip_group_check=True)
                        pe.wait_ge(doubled, c + 1)
                        for m in range(4):
                            b = 4 * c + m
                            mm = pe.matmul(dist[c][:, m * P:(m + 1) * P], ctxT_all[:, b * P:(b + 1) * P],
                                           xm2[:, b * P:(b + 1) * P], start=False, stop=True,
                                           skip_group_check=True)
                        mm.then_inc(dist_made, 1)

                @block.scalar
                def _(act):
                    for c in range(4):
                        act.wait_ge(turned, c + 1)
                        act.activation(chunk(xsq, c), turn[c][:, :], ACT.Square).then_inc(squared, 1)
                    for b in range(NB):
                        act.activation(csq[:, b * D:(b + 1) * D], ctx_all[:, b * D:(b + 1) * D], ACT.Square,
                                       accum_out=norm[:, b:b + 1]).then_inc(norm_step, 1)
                    act.preload_act_table(ACT.Sqrt)
                    for c in range(4):
                        act.wait_ge(a_ready, 4 * c + 4)
                        act.activation(chunk(s, c), chunk(a, c), ACT.Sqrt).then_inc(s_ready, 1)
                    for c in range(4):
                        act.activation(chunk(inv, c), chunk(a, c), ACT.Abs_reciprocal_sqrt)\
                           .then_inc(inv_ready, 1)

                @block.vector
                def _(dve):
                    for c in range(4):
                        dve.wait_ge(turned, c + 1)
                        dve.wait_ge(squared, c + 1)
                        dve.tensor_scalar(chunk(xm2, c), turn[c][:, :], -2.0, None, ALU.mult)\
                           .then_inc(doubled, 1)
                    dve.wait_ge(norm_step, NB)
                    for c in range(4):
                        dve.wait_ge(dist_made, c + 1)
                        for m in range(4):
                            b = 4 * c + m
                            dve.tensor_scalar(a[:, b * P:(b + 1) * P], dist[c][:, m * P:(m + 1) * P],
                                              norm[:, b:b + 1], 0.0, ALU.add, ALU.max).then_inc(a_ready, 1)
                    for c in range(4):
                        dve.wait_ge(s_ready, c + 1)
                        dve.tensor_tensor(chunk(sq, c), chunk(s, c), chunk(s, c), op=ALU.mult)\
                           .then_inc(sq_ready, 1)
                    for c in range(4):
                        dve.wait_ge(r_ready, c + 1)
                        dve.wait_ge(inv_ready, c + 1)
                        dve.scalar_tensor_tensor(chunk(inv, c), chunk(inv, c), 1e18, chunk(sq, c),
                                                 ALU.min, ALU.mult).then_inc(fix_ready, 1)
                        dve.wait_ge(fix_ready, c + 1)
                        dve.scalar_tensor_tensor(chunk(a, c), chunk(inv, c), 0.5, chunk(s, c),
                                                 ALU.mult, ALU.add).then_inc(d_ready, 1)

                @block.gpsimd
                def _(pool):
                    for c in range(4):
                        pool.wait_ge(sq_ready, c + 1)
                        pool.tensor_tensor(chunk(sq, c), chunk(a, c), chunk(sq, c), op=ALU.subtract)\
                            .then_inc(r_ready, 1)

                @block.sync
                def _(sp):
                    for c in range(4):
                        sp.wait_ge(d_ready, c + 1)
                        sp.dma_start(dist_dram[4 * c:4 * c + 4].rearrange("b i j -> i b j"),
                                     chunk(a, c).rearrange("i (b j) -> i b j", b=4)).then_inc(d_stored, 16)
                    sp.wait_ge(d_stored, 64)
                    sp.wait_ge(*later_loads)

        jump = sb("jump", [P, NB * P])
        last = sb("last", [P, NB * P])
        col = sb("col", [P, NB * P])
        choice = ExitStack()
        here = sb("here", [P, NB, R1], choice)
        above = sb("above", [P, NB, R1], choice)
        with ExitStack() as part:
            cost = sb("cost", [NB, R1 * R1], part)
            low = [sb(f"low{i}", [NB, P], part) for i in range(2)]
            rows = cost[:, :].rearrange("b (i j) -> b i j", j=R1)
            d_loaded, edges = [sem(f"d_loaded{i}") for i in range(len(BLOCKS))], sem("edges")
            low_ready, row_ready, cost_stored = sem("low_ready"), sem("row_ready"), sem("cost_stored")
            cost_loaded, col_ready = sem("cost_loaded"), sem("col_ready")
            side = later_work(part, sem)
            with nc.Block() as block:
                @block.sync
                def _(sp):
                    for n, (i0, i1) in enumerate(BLOCKS):
                        sp.dma_start(rows[:, 1 + i0:1 + i1, 1:R1], dist_dram[:, i0:i1, :])\
                          .then_inc(d_loaded[n], 16)
                    sp.wait_ge(edges, 3)
                    sp.dma_start(cost_dram[:, 0, :], rows[:, 0, :]).then_inc(cost_stored, 16)
                    for n, (i0, i1) in enumerate(BLOCKS):
                        sp.wait_ge(row_ready, i1)
                        sp.dma_start(cost_dram[:, 1 + i0:1 + i1, :], rows[:, 1 + i0:1 + i1, :])\
                          .then_inc(cost_stored, 16)
                        sp.wait_ge(cost_stored, 16 * (n + 2))
                        sp.dma_start(here[i0:i1, :, :], cost_dram[:, 1 + i0:1 + i1, :]
                                     .rearrange("b i j -> i b j")).then_inc(cost_loaded, 16)
                        sp.dma_start(above[i0:i1, :, :], cost_dram[:, i0:i1, :]
                                     .rearrange("b i j -> i b j")).then_inc(cost_loaded, 16)
                    sp.wait_ge(cost_loaded, 32 * len(BLOCKS))

                @block.tensor
                def _(pe):
                    side.tensor(pe)

                @block.scalar
                def _(act):
                    side.scalar(act)

                @block.gpsimd
                def _(pool):
                    side.gpsimd(pool)
                    pool.iota(col[:, :].rearrange("p (b j) -> p b j", b=NB), pattern=[[256, NB], [1, P]],
                              base=1, channel_multiplier=0,
                              allow_small_or_imprecise_dtypes=True).then_inc(col_ready, 1)

                @block.vector
                def _(dve):
                    dve.memset(rows[:, 0, :], BIG).then_inc(edges, 1)
                    dve.memset(rows[:, 1:R1, 0:1], BIG).then_inc(edges, 1)
                    dve.memset(low[0][:, :], BIG).then_inc(edges, 1)
                    dve.wait_ge(edges, 3)

                    for i in range(P):
                        for n, (i0, _) in enumerate(BLOCKS):
                            if i == i0:
                                dve.wait_ge(d_loaded[n], 16)
                        if i > 0:
                            dve.wait_ge(row_ready, i)
                            dve.tensor_tensor(low[i % 2][:, :], cost[:, i * R1 + 1:(i + 1) * R1],
                                              cost[:, i * R1:i * R1 + P], op=ALU.min)\
                               .then_inc(low_ready, 1)
                            dve.wait_ge(low_ready, i)
                        here_row = cost[:, (i + 1) * R1 + 1:(i + 2) * R1]
                        dve.tensor_tensor_scan(here_row, low[i % 2][:, :], here_row,
                                               BIG if i else 0.0, ALU.min, ALU.add).then_inc(row_ready, 1)

        with ExitStack() as part:
            low = sb("lowest", [P, NB, P], part)
            leaves = sb("leaves", [P, NB, P], part)
            diag = sb("diag", [P, NB, P], part)
            step, pool_step = sem("choice_step"), sem("choice_pool_step")
            jump_ready, jump_stored, last_ready = sem("jump_ready"), sem("jump_stored"), sem("last_ready")
            HALVES = [slice(0, NB // 2), slice(NB // 2, NB)]

            def compare(dve, bs, base):
                up, corner, left = above[:, bs, 1:R1], above[:, bs, 0:P], here[:, bs, 0:P]
                dve.tensor_tensor(diag[:, bs, :], corner, up, op=ALU.is_le).then_inc(step, 1)
                dve.tensor_tensor(low[:, bs, :], corner, up, op=ALU.min).then_inc(step, 1)
                dve.wait_ge(step, base + 2)
                dve.tensor_tensor(leaves[:, bs, :], low[:, bs, :], left, op=ALU.is_le).then_inc(step, 1)

            def columns(eng, bs, done, base):
                col3 = col[:, :].rearrange("p (b j) -> p b j", b=NB)[:, bs, :]
                eng.tensor_tensor(leaves[:, bs, :], leaves[:, bs, :], col3, op=ALU.mult).then_inc(done, 1)
                eng.wait_ge(done, base + 1)
                eng.tensor_tensor(low[:, bs, :], leaves[:, bs, :], diag[:, bs, :], op=ALU.subtract)\
                   .then_inc(done, 1)

            with nc.Block() as block:
                def store(eng, i0, i1):
                    eng.wait_ge(jump_ready, 1)
                    eng.dma_start(jump_dram[:, i0:i1, :].rearrange("b i j -> i b j"),
                                  jump[i0:i1, :].rearrange("i (b j) -> i b j", b=NB)).then_inc(jump_stored, 16)

                @block.sync
                def _(sp):
                    store(sp, P // 2, P)
                    sp.wait_ge(jump_stored, 32)

                @block.scalar
                def _(act):
                    store(act, 0, P // 2)

                @block.gpsimd
                def _(pool):
                    pool.wait_ge(step, 3)
                    columns(pool, HALVES[0], pool_step, 0)

                @block.vector
                def _(dve):
                    compare(dve, HALVES[0], 0)
                    compare(dve, HALVES[1], 3)
                    dve.wait_ge(step, 6)
                    columns(dve, HALVES[1], step, 6)
                    dve.wait_ge(step, 8)
                    dve.wait_ge(pool_step, 2)
                    n = low[:, :, :].rearrange("p b j -> p (b j)")
                    l = leaves[:, :, :].rearrange("p b j -> p (b j)")
                    dve.tensor_tensor_scan(jump[:, :], n, n, 0.0, ALU.max, ALU.max).then_inc(jump_ready, 1)
                    dve.tensor_tensor_scan(last[:, :], l, l, 0.0, ALU.max, ALU.max).then_inc(last_ready, 1)
        choice.close()

        enter = sb("enter", [NB, P])
        with ExitStack() as part:
            table = sb("table", [NB, P * P], part)
            junk = sb("junk", [NB, P], part)
            col_b = sb("col_b", [NB, P], part)
            BACK = [(120, 128), (96, 120), (64, 96), (0, 64)]
            table_loaded = [sem(f"table_loaded{n}") for n in range(len(BACK))]
            col_ready, entered = sem("col_b_ready"), sem("entered")
            with nc.Block() as block:
                @block.sync
                def _(sp):
                    for n, (i0, i1) in enumerate(BACK):
                        sp.dma_start(table[:, i0 * P:i1 * P],
                                     jump_dram[:, i0:i1, :].rearrange("b i j -> b (i j)"))\
                          .then_inc(table_loaded[n], 16)

                @block.gpsimd
                def _(pool):
                    pool.iota(col_b[:, :], pattern=[[1, P]], base=1, channel_multiplier=256,
                              allow_small_or_imprecise_dtypes=True).then_inc(col_ready, 1)

                @block.vector
                def _(dve):
                    dve.wait_ge(col_ready, 1)
                    dve.tensor_copy(enter[:, P - 1:P], col_b[:, P - 1:P]).then_inc(entered, 1)

                    def step(k):
                        i = P - 1 - k
                        for n, (_, i1) in enumerate(BACK):
                            if i == i1 - 1:
                                dve.wait_ge(table_loaded[n], 16)
                        wait(dve, entered, k + 1)
                        dve.scalar_tensor_tensor(junk[:, :], col_b[:, :], enter[:, i:i + 1],
                                                 table[:, i * P:(i + 1) * P], ALU.is_equal, ALU.mult,
                                                 accum_out=enter[:, i - 1:i])\
                           .then_inc(entered, 1)

                    for k in range(P - 1):
                        step(k)

        with ExitStack() as part:
            hi = sb("hi", [P, NB], part)
            lo = sb("lo", [P, NB], part)
            junk = sb("junk5", [P, NB * P], part)
            below = sb("below", [P, NB * P], part)
            z = sb("z", [P, NB * D], part)
            hi_bank = part.enter_context(nc.psum_tensor("dtw_hi_bank", [P, SPAN], FP32))
            add = [part.enter_context(nc.psum_tensor(f"dtw_add{i}", [P, SPAN], FP32)) for i in range(4)]
            hi_made, hi_ready, lo_ready = sem("hi_made"), sem("hi_ready"), sem("lo_ready")
            below_ready, above_ready, path_ready = sem("below_ready"), sem("above_ready"), sem("path_ready")
            added, z_ready = sem("added"), sem("z_ready")

            def wide(t, n):
                return spread(t[:, :], [P, NB, n])

            with nc.Block() as block:
                @block.tensor
                def _(pe):
                    pe.matmul(hi_bank[:, 0:NB], enter[:, :], consts["ident"][0:NB, 0:NB], start=True,
                              stop=True).then_inc(hi_made, 1)
                    for c in range(4):
                        pe.wait_ge(path_ready, c + 1)
                        for m in range(4):
                            b = 4 * c + m
                            mm = pe.matmul(add[c][:, m * D:(m + 1) * D], junk[:, b * P:(b + 1) * P],
                                           ctx_all[:, b * D:(b + 1) * D], start=True, stop=True)
                        mm.then_inc(added, 1)

                @block.vector
                def _(dve):
                    dve.wait_ge(hi_made, 1)
                    dve.tensor_copy(hi[:, :], hi_bank[:, 0:NB]).then_inc(hi_ready, 1)
                    dve.wait_ge(hi_ready, 1)
                    for b in range(NB):
                        dve.scalar_tensor_tensor(junk[:, b * P:(b + 1) * P], col[:, b * P:(b + 1) * P],
                                                 hi[:, b:b + 1], last[:, b * P:(b + 1) * P],
                                                 ALU.is_equal, ALU.mult, accum_out=lo[:, b:b + 1])\
                           .then_inc(lo_ready, 1)
                    for c in range(4):
                        cols, bs = slice(c * SPAN, (c + 1) * SPAN), slice(4 * c, 4 * c + 4)
                        col3 = col[:, cols].rearrange("p (b j) -> p b j", b=4)
                        dve.tensor_tensor(below[:, cols].rearrange("p (b j) -> p b j", b=4), col3,
                                          spread(hi[:, bs], [P, 4, P]), op=ALU.is_le)\
                           .then_inc(below_ready, 1)
                        dve.wait_ge(lo_ready, NB)
                        dve.tensor_tensor(junk[:, cols].rearrange("p (b j) -> p b j", b=4), col3,
                                          spread(lo[:, bs], [P, 4, P]), op=ALU.is_ge)\
                           .then_inc(above_ready, 1)
                        dve.wait_ge(below_ready, c + 1)
                        dve.wait_ge(above_ready, c + 1)
                        dve.tensor_tensor(junk[:, cols], junk[:, cols], below[:, cols], op=ALU.mult)\
                           .then_inc(path_ready, 1)
                    for c in range(4):
                        dve.wait_ge(added, c + 1)
                        dve.tensor_tensor(z[:, c * SPAN:(c + 1) * SPAN], add[c][:, :],
                                          x_all[:, c * SPAN:(c + 1) * SPAN], op=ALU.add).then_inc(z_ready, 1)

            layer_norm_all(nc, "dtw", consts, z, x_all)


def turn_all(nc, name, consts, x_all, xT_all):
    with ExitStack() as ctx:
        banks = [ctx.enter_context(nc.psum_tensor(f"{name}_turn{i}", [P, SPAN], FP32)) for i in range(4)]
        turned = ctx.enter_context(nc.semaphore(f"{name}_turned"))
        moved = ctx.enter_context(nc.semaphore(f"{name}_moved"))
        with nc.Block() as block:
            @block.tensor
            def _(pe):
                for b in range(NB):
                    mm = pe.transpose(banks[b // 4][:, b % 4 * P:(b % 4 + 1) * P],
                                      x_all[:, b * D:(b + 1) * D], consts["ident"])
                    if b % 4 == 3:
                        mm.then_inc(turned, 1)

            @block.scalar
            def _(act):
                for c in (0, 2):
                    act.wait_ge(turned, c + 1)
                    act.activation(xT_all[:, c * SPAN:(c + 1) * SPAN], banks[c][:, :], ACT.Copy)\
                       .then_inc(moved, 1)

            @block.vector
            def _(dve):
                for c in (1, 3):
                    dve.wait_ge(turned, c + 1)
                    dve.tensor_copy(xT_all[:, c * SPAN:(c + 1) * SPAN], banks[c][:, :]).then_inc(moved, 1)


def experts_stage(nc, consts, weights, x_all, load_next, next_v):
    with ExitStack() as ctx:
        sem = ctx.enter_context(stage_semaphores(nc, "moe"))

        def sb(name, shape, dt=FP32):
            return ctx.enter_context(nc.sbuf_tensor(f"moe_{name}", shape, dt))

        xT = sb("xT", [P, NB * P])
        x_lead, x_left = sb("x_lead", [P, NB * P], FP32R), sb("x_left", [P, NB * P], FP32R)
        fc_left, fc_last_left = sb("fc_left", [P, N_EXP * D_FF], FP32R), sb("fc_last_left", [P, N_EXP * P], FP32R)
        GE = NB * N_EXP
        gate = sb("gate", [P, NB, N_EXP])
        z = sb("z", [P, NB * D])

        with ExitStack() as part:
            up = [[part.enter_context(nc.psum_tensor(f"moe_{n}{u}", [P, SPAN], FP32)) for n in "ag"]
                  for u in range(3)]
            down = [part.enter_context(nc.psum_tensor(f"moe_down{e}", [P, SPAN], FP32)) for e in range(2)]
            act_a = [part.enter_context(nc.sbuf_tensor(f"moe_act{u}", [P, SPAN], FP32)) for u in range(3)]
            h = [[part.enter_context(nc.sbuf_tensor(f"moe_h{p}{u}", [P, SPAN], FP32)) for u in range(3)]
                 for p in range(2)]
            unit_made, silu_ready, h_ready = sem("unit_made"), sem("silu_ready"), sem("h_ready")
            down_made, summed = sem("down_made"), sem("summed")

            def pb(name, shape, dt=FP32):
                return part.enter_context(nc.sbuf_tensor(f"gate_{name}", shape, dt))

            turn_banks, logits, place = [up[1][0], up[1][1], up[2][0], up[2][1]], down[0], down[1]
            top = pb("top", [P, NB])
            e = pb("e", [P, NB, N_EXP])
            total = pb("total", [P, NB])
            best = pb("best", [P, NB, 8])
            index = pb("index", [P, NB, 8], mybir.dt.uint32)
            chosen = pb("chosen", [P, NB, 8])
            one = pb("one", [P, 2, NB, N_EXP])
            picks = pb("picks", [P, NB, N_EXP])
            PAD = 8
            before = [pb(f"before{i}", [P, PAD + NB, N_EXP]) for i in range(2)]
            fits = pb("fits", [P, NB, N_EXP])
            logits_made, shifted, exped, step = sem("logits"), sem("shifted"), sem("exped"), sem("step")
            placed, counted, gate_ready = sem("placed"), sem("counted"), sem("gate_ready")
            cleared = sem("cleared")
            turned, moved = sem("turned"), sem("moved")
            fc_ready = sem("fc_ready")
            led, left, next_loaded, next_led = sem("led"), sem("left"), sem("next_loaded"), sem("next_led")
            logits3 = logits[:, 0:GE].rearrange("p (b e) -> p b e", b=NB)
            PAIRS = N_EXP // 2
            fc = weights["L0_ffn_c_fc"]
            gate2 = gate[:, :, :].rearrange("p b e -> p (b e)")

            def turns(eng, turn, after_first=None):
                for pair in range(PAIRS):
                    turn(0, pair, pair > 0, True)
                    if pair == 0 and after_first:
                        after_first()
                with eng.Fori(1, NB // 4) as c:
                    for pair in range(PAIRS):
                        turn(c, pair, True, True)
                turn(NB // 4, 0, True, False)

            with nc.Block() as block:
                @block.sync
                def _(sp):
                    load_next(sp, next_loaded)

                @block.gpsimd
                def _(pool):
                    for c in range(4):
                        for name, lead, rest, n in (("L0_ffn_c_fc", "fc_lead", fc_left, 2 * D_FF),
                                                    ("fc_last", "fc_last_lead", fc_last_left, 2 * P)):
                            cols = slice(c * n, (c + 1) * n)
                            pool.tensor_tensor(rest[:, cols], weights[name][:, cols],
                                               weights[lead][:, cols].bitcast(FP32),
                                               op=ALU.subtract).then_inc(fc_ready, 1)
                        cols = slice(c * SPAN, (c + 1) * SPAN)
                        pool.wait_ge(led, c + 1)
                        pool.tensor_tensor(x_left[:, cols], xT[:, cols], x_lead[:, cols].bitcast(FP32),
                                           op=ALU.subtract).then_inc(left, 1)
                    whole, lead, rest = next_v
                    pool.wait_ge(next_loaded, NEXT_LOADS * 16)
                    pool.tensor_copy(lead, whole).then_inc(next_led, 1)
                    pool.wait_ge(next_led, 1)
                    pool.tensor_tensor(rest, whole, lead.bitcast(FP32), op=ALU.subtract).then_inc(next_led, 1)

                @block.tensor
                def _(pe):
                    def columns(pair, u, half):
                        if u < 2:
                            at = (2 * pair + u) * D_FF + half * HALF
                            return weights["fc_lead"][:, at:at + P], fc_left[:, at:at + P]
                        at = (2 * pair + half) * P
                        return weights["fc_last_lead"][:, at:at + P], fc_last_left[:, at:at + P]

                    def turn(c, pair, earlier, present):
                        k = c * PAIRS + pair
                        if present:
                            for u in range(3):
                                if isinstance(c, int) and u == 0:
                                    pe.wait_ge(fc_ready, 2 * pair + 2)
                                if not earlier and u == 0:
                                    pe.wait_ge(led, 4)
                                    pe.wait_ge(left, 1)
                                if isinstance(c, int) and pair == PAIRS - 1 and u == 0:
                                    pe.wait_ge(left, 4)
                                wait(pe, h_ready, 3 * k + u - 2)
                                tokens = bass.ds(c * SPAN, SPAN)
                                for half in range(2):
                                    w_lead, w_left = columns(pair, u, half)
                                    bank = up[u][half][:, :]
                                    pe.matmul(bank, w_lead, x_lead[:, tokens], start=True, stop=False)
                                    pe.matmul(bank, w_lead, x_left[:, tokens], start=False, stop=False)
                                    mm = pe.matmul(bank, w_left, x_lead[:, tokens], start=False, stop=True)
                                mm.then_inc(unit_made, 1)
                        if earlier:
                            before, p = (pair - 1) % PAIRS, (pair - 1) % 2
                            wait(pe, h_ready, 3 * k)
                            for e in range(2):
                                if isinstance(c, int) and k == 1:
                                    pe.wait_ge(gate_ready, 2)
                                wait(pe, summed, (k - 2) * 8 + (e + 1) * 4)
                                first = weights["proj_first"][:, (2 * before + e) * D:(2 * before + e + 1) * D]
                                last = weights["proj_last"][64 * e:64 * e + 64, before * D:(before + 1) * D]
                                for m in range(4):
                                    cols = slice(m * P, (m + 1) * P)
                                    pe.matmul(down[e][:, cols], h[p][e][:, cols], first,
                                              start=True, stop=False)
                                    mm = pe.matmul(down[e][:, cols], h[p][2][64 * e:64 * e + 64, cols],
                                                   last, start=False, stop=True)
                                mm.then_inc(down_made, 1)

                    for c in range(4):
                        for m in range(4):
                            b = 4 * c + m
                            mm = pe.transpose(turn_banks[c][:, m * P:(m + 1) * P],
                                              x_all[:, b * D:(b + 1) * D], consts["ident"])
                        mm.then_inc(turned, 1)
                    for c in range(4):
                        pe.wait_ge(moved, c + 1)
                        for b in range(4 * c, 4 * c + 4):
                            mm = pe.matmul(logits[:, b * N_EXP:(b + 1) * N_EXP], xT[:, b * P:(b + 1) * P],
                                           weights["L0_ffn_w_gate"][:, :], start=True, stop=True)
                    mm.then_inc(logits_made, 1)

                    def places():
                        pe.wait_ge(counted, 1)
                        pe.matmul(place[:, 0:GE], consts["before"], picks[:, :, :], start=True, stop=False)
                        pe.matmul(place[:, 0:GE], consts["ones"], before[0][:, PAD:, :], start=False,
                                  stop=True).then_inc(placed, 1)

                    turns(pe, turn, places)

                @block.scalar
                def _(act):
                    act.preload_act_table(ACT.Exp)
                    for c in range(4):
                        act.wait_ge(turned, c + 1)
                        act.activation(xT[:, c * SPAN:(c + 1) * SPAN], turn_banks[c][:, :], ACT.Copy)\
                           .then_inc(moved, 1)
                    act.wait_ge(shifted, 1)
                    act.activation(e[:, :, :], e[:, :, :], ACT.Exp).then_inc(exped, 1)
                    act.preload_act_table(ACT.Silu)

                    def turn(c, pair, earlier, present):
                        k = c * PAIRS + pair
                        if present:
                            for u in range(3):
                                wait(act, unit_made, 3 * k + u + 1)
                                act.activation(act_a[u][:, :], up[u][0][:, :], ACT.Silu)\
                                   .then_inc(silu_ready, 1)

                    turns(act, turn)

                @block.vector
                def _(dve):
                    def turn(c, pair, earlier, present):
                        k = c * PAIRS + pair
                        if present:
                            for u in range(3):
                                wait(dve, silu_ready, 3 * k + u + 1)
                                wait(dve, down_made, 2 * k - 2)
                                dve.tensor_tensor(h[pair % 2][u][:, :], act_a[u][:, :], up[u][1][:, :],
                                                  op=ALU.mult).then_inc(h_ready, 1)
                        if earlier:
                            before = (pair - 1) % PAIRS
                            cb = c if pair else c - 1
                            for e in range(2):
                                wait(dve, down_made, 2 * k - 1 + e)
                                for m in range(4):
                                    b = cb * 4 + m
                                    zb = z[:, bass.ds(b * D, D)]
                                    base = x_all[:, bass.ds(b * D, D)] if before + e == 0 else zb
                                    if before + e > 0:
                                        wait(dve, summed, (k - 1) * 8 + e * 4 + m - 3)
                                    dve.scalar_tensor_tensor(
                                        zb, down[e][:, m * D:(m + 1) * D],
                                        gate2[:, bass.ds(b * N_EXP + 2 * before + e, 1)], base,
                                        ALU.mult, ALU.add).then_inc(summed, 1)

                    link = linker(dve, step)
                    for i in range(2):
                        dve.memset(before[i][:, 0:PAD + 1, :], 0.0).then_inc(cleared, 1)
                    for c in range(4):
                        dve.wait_ge(moved, c + 1)
                        dve.tensor_copy(x_lead[:, c * SPAN:(c + 1) * SPAN], xT[:, c * SPAN:(c + 1) * SPAN])\
                           .then_inc(led, 1)
                    dve.wait_ge(logits_made, 1)
                    link(dve.tensor_reduce(top[:, :], logits3, AX.X, ALU.max))
                    dve.tensor_tensor(e[:, :, :], logits3, spread(top[:, :], [P, NB, N_EXP]),
                                      op=ALU.subtract).then_inc(shifted, 1)
                    dve.wait_ge(exped, 1)
                    link(dve.tensor_reduce(total[:, :], e[:, :, :], AX.X, ALU.add))
                    link(dve.reciprocal(total[:, :], total[:, :]))
                    link(dve.tensor_tensor(e[:, :, :], e[:, :, :], spread(total[:, :], [P, NB, N_EXP]),
                                           op=ALU.mult))
                    for b in range(NB):
                        ins = dve.max(best[:, b, :], e[:, b, :])
                    link(ins)
                    for b in range(NB):
                        ins = dve.max_index(index[:, b, :], best[:, b, :], e[:, b, :])
                    link(ins)
                    link(dve.tensor_copy(chosen[:, :, :], index[:, :, :]))
                    for k in range(2):
                        ins = dve.tensor_tensor(one[:, k, :, :],
                                                consts["iota8"].rearrange("p (o e) -> p o e", o=1)
                                                .broadcast_to([P, NB, N_EXP]),
                                                chosen[:, :, k:k + 1].broadcast_to([P, NB, N_EXP]),
                                                op=ALU.is_equal)
                    link(ins)
                    link(dve.tensor_tensor(picks[:, :, :], one[:, 0, :, :], one[:, 1, :, :], op=ALU.add))
                    dve.wait_ge(cleared, 2)
                    link(dve.tensor_copy(before[0][:, PAD + 1:, :], picks[:, 0:NB - 1, :]))
                    for n, reach in enumerate((1, 2, 4, 8)):
                        src, dst = before[n % 2], before[1 - n % 2]
                        ins = dve.tensor_tensor(dst[:, PAD:, :], src[:, PAD:, :],
                                                src[:, PAD - reach:PAD + NB - reach, :], op=ALU.add)
                        if reach < 8:
                            link(ins)
                    ins.then_inc(counted, 1)

                    def finish_gate():
                        dve.tensor_tensor(e[:, :, :], e[:, :, :], picks[:, :, :], op=ALU.mult)\
                           .then_inc(gate_ready, 1)
                        dve.wait_ge(placed, 1)
                        dve.tensor_scalar(fits[:, :, :], place[:, 0:GE].rearrange("p (b e) -> p b e", b=NB),
                                          float(CAPACITY), None, ALU.is_lt).then_inc(gate_ready, 1)
                        dve.wait_ge(gate_ready, 2)
                        dve.tensor_tensor(gate[:, :, :], e[:, :, :], fits[:, :, :], op=ALU.mult)\
                           .then_inc(gate_ready, 1)
                        dve.wait_ge(gate_ready, 3)

                    turns(dve, turn, finish_gate)

        layer_norm_all(nc, "moe", consts, z, x_all)


class LaterWork:

    def __init__(self, nc, part, sem, consts, weights, ctxT_all, turned, kT_all, v_all):
        self.consts, self.weights, self.ctxT_all = consts, weights, ctxT_all
        self.turned, self.kT_all, self.v_all = turned, kT_all, v_all
        self.wo = part.enter_context(nc.sbuf_tensor("later_wo", [P, 4 * P], FP32))
        self.sin_part = part.enter_context(nc.sbuf_tensor("later_sin", [P, SPAN], FP32))
        self.banks = [part.enter_context(nc.psum_tensor(f"later{i}", [P, SPAN], FP32)) for i in range(8)]
        self.wo_cleared, self.wo_spread = sem("wo_cleared"), sem("wo_spread")
        self.w_turned, self.w_moved, self.swapped = sem("w_turned"), sem("w_moved"), sem("swapped")
        self.made, self.moved = sem("kv_made"), sem("kv_moved")
        self.steps = sem("kv_steps")
        self.led = sem("fc_led")

    def tensor(self, pe):
        for n, (name, blocks) in enumerate(LATER):
            if name == "L1_xattn_Wo":
                pe.wait_ge(self.wo_spread, 1)
            if n >= 4:
                pe.wait_ge(self.w_moved, n - 3)
            src = self.wo if name == "L1_xattn_Wo" else self.weights[name]
            for m in range(blocks):
                mm = pe.transpose(self.banks[n % 4][:, m * P:(m + 1) * P], src[:, m * P:(m + 1) * P],
                                  self.consts["ident"])
            mm.then_inc(self.w_turned, 1)
        pe.wait_ge(self.w_moved, len(LATER))
        pe.wait_ge(self.swapped, 2)
        for c in range(4):
            cols = self.ctxT_all[:, c * SPAN:(c + 1) * SPAN]
            if c > 1:
                pe.wait_ge(self.moved, 3 * (c - 1))
            k, kt, v = self.banks[0 + c % 2], self.banks[2 + c % 2], self.banks[4 + c % 2]
            pe.matmul(k[:, :], self.weights["L1_xattn_Wk"][:, :], cols, start=True, stop=True)\
              .then_inc(self.made, 1)
            pe.matmul(kt[:, :], self.turned[0], cols, start=True, stop=True).then_inc(self.made, 1)
            for m in range(4):
                b = 4 * c + m
                mm = pe.matmul(v[:, m * P:(m + 1) * P], self.ctxT_all[:, b * P:(b + 1) * P],
                               self.weights["L1_xattn_Wv"][:, :], start=True, stop=True)
            mm.then_inc(self.made, 1)

    def fc_chunks(self):
        for name, n in (("L0_ffn_c_fc", N_EXP * D_FF), ("fc_last", N_EXP * P)):
            lead = self.weights["fc_lead" if name == "L0_ffn_c_fc" else "fc_last_lead"]
            for first in range(0, n, SPAN):
                yield self.weights[name][:, first:first + SPAN], lead[:, first:first + SPAN]

    def scalar(self, act):
        for n, (name, blocks) in enumerate(LATER):
            act.wait_ge(self.w_turned, n + 1)
            act.activation(self.weights[name][:, :], self.banks[n % 4][:, 0:blocks * P], ACT.Copy)\
               .then_inc(self.w_moved, 1)
            if n == 1:
                act.wait_ge(self.w_moved, 2)
                for i, (w, _) in enumerate(LATER[0:2]):
                    src = self.weights[w][:, :].rearrange("p (h s d) -> p h s d", h=16, s=2)
                    dst = self.turned[i].rearrange("p (h s d) -> p h s d", h=16, s=2)
                    for half in range(2):
                        act.activation(dst[:, :, half, :], src[:, :, 1 - half, :], ACT.Copy)\
                           .then_inc(self.swapped, 1)
        for c in range(4):
            out = slice(c * SPAN, (c + 1) * SPAN)
            act.wait_ge(self.made, 3 * c + 1)
            act.activation(self.kT_all[:, out], self.banks[0 + c % 2][:, :], ACT.Identity,
                           bias=self.weights["L1_xattn_bk"]).then_inc(self.moved, 1)
            act.wait_ge(self.made, 3 * c + 2)
            wait(act, self.steps, 4 * c)
            act.activation(self.sin_part[:, :], self.banks[2 + c % 2][:, :], ACT.Identity,
                           bias=self.weights["L1_xattn_bk_turned"]).then_inc(self.moved, 1)
            act.wait_ge(self.made, 3 * c + 3)
            act.activation(self.v_all[:, out], self.banks[4 + c % 2][:, :], ACT.Copy).then_inc(self.moved, 1)
        for whole, lead in self.fc_chunks():
            act.activation(lead, whole, ACT.Copy).then_inc(self.led, 1)

    def gpsimd(self, pool):
        pool.memset(self.wo[:, :], 0.0).then_inc(self.wo_cleared, 1)
        pool.wait_ge(self.wo_cleared, 1)
        pool.tensor_copy(self.wo[:, :].rearrange("p (h d) -> p h d", d=32)[:, :, 0:8],
                         self.weights["L1_xattn_Wo"][:, 0:P].rearrange("p (h d) -> p h d", d=8))\
            .then_inc(self.wo_spread, 1)

        def repeated(t):
            return t.rearrange("p (o j) -> p o j", o=1).broadcast_to([P, 4, P])

        for c in range(4):
            out = slice(c * SPAN, (c + 1) * SPAN)
            k, kt, v = (t.rearrange("p (b j) -> p b j", b=4)
                        for t in (self.kT_all[:, out], self.sin_part[:, :], self.v_all[:, out]))
            pool.wait_ge(self.moved, 3 * c + 3)
            pool.tensor_tensor(k, k, repeated(self.consts["cos"]), op=ALU.mult).then_inc(self.steps, 1)
            pool.tensor_tensor(kt, kt, repeated(self.consts["sin"]), op=ALU.mult).then_inc(self.steps, 1)
            pool.wait_ge(self.steps, 4 * c + 2)
            pool.tensor_tensor(k, k, kt, op=ALU.add).then_inc(self.steps, 1)
            pool.tensor_tensor(v, v, repeated(self.weights["L1_xattn_bv"]), op=ALU.add)\
                .then_inc(self.steps, 1)


def recurrent_stage(nc, consts, weights, x_all, xT):
    with ExitStack() as ctx:
        sem = ctx.enter_context(stage_semaphores(nc, "rnn"))

        def sb(name, shape):
            return ctx.enter_context(nc.sbuf_tensor(f"rnn_{name}", shape, FP32))

        z = sb("z", [P, NB * D])
        c_state = [sb(f"c{i}", [P, P]) for i in range(2)]
        gates = [sb(f"gates{i}", [P, 3, P]) for i in range(2)]
        parts = [sb(f"parts{i}", [P, 2, P]) for i in range(2)]
        common = sb("common", [P, D])
        hidden = sb("hidden", [P, NB * D])
        banks = [[ctx.enter_context(nc.psum_tensor(f"rnn_b{i}{n}", [P, SPAN], FP32)) for n in range(3)]
                 for i in range(2)]
        outs = [ctx.enter_context(nc.psum_tensor(f"rnn_o{i}", [P, SPAN], FP32)) for i in range(2)]
        gates_made, gates_ready, products, c_ready = sem("gates_made"), sem("gates_ready"), sem("products"), sem("c_ready")
        out_made, out_moved, tanh_ready, z_ready = sem("out_made"), sem("out_moved"), sem("tanh"), sem("z")
        W = ("wf", "wi", "wc")
        U = ("uf", "ui", "uc")
        with nc.Block() as block:
            @block.tensor
            def _(pe):
                def step(t, p, first=False):
                    for n in range(3):
                        if not first:
                            wait(pe, gates_ready, 3 * (t - 2) + n + 1)
                        pe.matmul(banks[p][n][:, 0:P], weights["L1_ffn_" + W[n]][:, :],
                                  xT[:, bass.ds(t * P, P)], start=True, stop=False)
                    wait(pe, c_ready, t + 1)
                    for n in range(3):
                        pe.matmul(banks[p][n][:, 0:P], weights["L1_ffn_" + U[n]][:, :],
                                  c_state[p][:, :], start=False, stop=True).then_inc(gates_made, 1)

                for t in range(2):
                    step(t, t, first=True)
                with pe.Fori(1, NB // 2) as k:
                    for u in range(2):
                        step(k * 2 + u, u)
                pe.wait_ge(c_ready, NB + 1)
                pe.matmul(outs[0][:, 0:D], c_state[0][:, :], weights["L1_ffn_uo"][:, :], start=True,
                          stop=True).then_inc(out_made, 1)
                for c in range(4):
                    wait(pe, out_moved, c)
                    for m in range(4):
                        b = 4 * c + m
                        mm = pe.matmul(outs[1 - c % 2][:, m * D:(m + 1) * D], xT[:, b * P:(b + 1) * P],
                                       weights["L1_ffn_wo"][:, :], start=True, stop=True)
                    mm.then_inc(out_made, 1)

            @block.scalar
            def _(act):
                act.preload_act_table_set("sigmoid_and_others")

                def step(t, p):
                    for n, (func, bias) in enumerate(((ACT.Sigmoid, "bf"), (ACT.Sigmoid, "bi"), (ACT.Tanh, "bc"))):
                        wait(act, gates_made, 3 * t + n + 1)
                        act.activation(gates[p][:, n, :], banks[p][n][:, 0:P], func,
                                       bias=weights["L1_ffn_" + bias]).then_inc(gates_ready, 1)

                for t in range(2):
                    step(t, t)
                with act.Fori(1, NB // 2) as k:
                    for u in range(2):
                        step(k * 2 + u, u)
                for c in range(4):
                    act.wait_ge(out_moved, c + 2)
                    act.activation(hidden[:, c * SPAN:(c + 1) * SPAN], z[:, c * SPAN:(c + 1) * SPAN],
                                   ACT.Tanh).then_inc(tanh_ready, 1)

            @block.vector
            def _(dve):
                dve.tensor_copy(c_state[0][:, :], weights["L1_ffn_in_c"].broadcast_to([P, P]))\
                   .then_inc(c_ready, 1)

                def step(t, p):
                    wait(dve, c_ready, t + 1)
                    wait(dve, gates_ready, 3 * t + 1)
                    dve.tensor_tensor(parts[p][:, 0, :], gates[p][:, 0, :], c_state[p][:, :], op=ALU.mult)\
                       .then_inc(products, 1)
                    wait(dve, gates_ready, 3 * t + 3)
                    dve.tensor_tensor(parts[p][:, 1, :], gates[p][:, 1, :], gates[p][:, 2, :], op=ALU.mult)\
                       .then_inc(products, 1)
                    wait(dve, products, 2 * t + 2)
                    dve.tensor_tensor(c_state[1 - p][:, :], parts[p][:, 0, :], parts[p][:, 1, :], op=ALU.add)\
                       .then_inc(c_ready, 1)

                for t in range(2):
                    step(t, t)
                with dve.Fori(1, NB // 2) as k:
                    for u in range(2):
                        step(k * 2 + u, u)
                dve.wait_ge(out_made, 1)
                dve.tensor_tensor(common[:, :], outs[0][:, 0:D], weights["L1_ffn_bo"], op=ALU.add)\
                   .then_inc(out_moved, 1)
                dve.wait_ge(out_moved, 1)
                for c in range(4):
                    dve.wait_ge(out_made, c + 2)
                    dve.tensor_tensor(z[:, c * SPAN:(c + 1) * SPAN].rearrange("p (b d) -> p b d", b=4),
                                      outs[1 - c % 2][:, :].rearrange("p (b d) -> p b d", b=4),
                                      common[:, :].rearrange("p (o d) -> p o d", o=1)
                                      .broadcast_to([P, 4, D]), op=ALU.add).then_inc(out_moved, 1)
                for c in range(4):
                    dve.wait_ge(tanh_ready, c + 1)
                    dve.tensor_tensor(z[:, c * SPAN:(c + 1) * SPAN], hidden[:, c * SPAN:(c + 1) * SPAN],
                                      x_all[:, c * SPAN:(c + 1) * SPAN], op=ALU.add).then_inc(z_ready, 1)

        layer_norm_all(nc, "rnn", consts, z, x_all)


FIRST = [("L0_attn_w_qkv", 24), ("L0_attn_w_out", 8)]
LATER = [("L1_xattn_Wk", 1), ("L1_xattn_Wq", 1), ("L1_xattn_Wv", 1), ("L1_xattn_Wo", 4),
         ("L1_ffn_wf", 1), ("L1_ffn_wi", 1), ("L1_ffn_wc", 1), ("L1_ffn_wo", 1),
         ("L1_ffn_uf", 1), ("L1_ffn_ui", 1), ("L1_ffn_uc", 1), ("L1_ffn_uo", 1)]
PLAIN = [("L0_ffn_w_gate", "p n -> p n", [P, N_EXP]),
         ("L0_ffn_c_fc", "e p n -> p e n", [P, N_EXP * D_FF])]
COLUMNS = ["L0_attn_ln_gamma", "L0_attn_ln_beta", "L1_xattn_bq", "L1_xattn_bk", "L1_ffn_bf",
           "L1_ffn_bi", "L1_ffn_bc", "L1_ffn_in_c"]
ROWS = ["L0_attn_b_out", "L1_attn_b_out", "L1_attn_ln_gamma", "L1_attn_ln_beta", "L1_xattn_bv",
        "L1_xattn_bo", "L1_ffn_bo"]


def load_later(sp, dram, weights, loaded):
    count = [0]

    def load(dst, src):
        sp.dma_start(dst, src).then_inc(loaded, 16)
        count[0] += 1

    for name, _ in LATER:
        load(weights[name][:, 0:P], dram[name])
    for name, how, _ in PLAIN:
        out = weights[name][:, :]
        if how != "p n -> p n":
            out = out.rearrange("p (c n) -> p c n", c=N_EXP)
        load(out, dram[name].rearrange(how))
    for e in range(2):
        load(weights["proj_last"][64 * e:64 * e + 64, :].rearrange("p (e d) -> p e d", d=P),
             dram["L0_ffn_c_proj"][e::2, P:HALF, :].rearrange("e p d -> p e d"))
        for half in range(2):
            load(weights["fc_last"][:, :].rearrange("p (i h e n) -> p i h e n", h=2, e=2,
                                                    n=64)[:, :, half, e, :],
                 dram["L0_ffn_c_fc"][e::2, :, half * HALF + P:(half + 1) * HALF]
                 .rearrange("i p n -> p i n"))
    load(weights["proj_first"][:, :].rearrange("p (e d) -> p e d", d=P),
         dram["L0_ffn_c_proj"][:, 0:P, :].rearrange("e p d -> p e d"))
    for name in COLUMNS[2:] + ["L1_xattn_bq_turned", "L1_xattn_bk_turned"]:
        load(weights[name], dram[name].rearrange("(p o) -> p o", o=1))
    for name in ROWS[1:]:
        load(weights[name], dram[name].rearrange("(o n) -> o n", o=1).broadcast_to([P, P]))
    return count[0]


NEXT_LOADS = 9


def load_second_attention(sp, dram, weights, loaded):
    sp.dma_start(weights["L1_attn_w_qkv"][:, :], dram["L1_attn_w_qkv"]).then_inc(loaded, 16)
    for n in range(4):
        for i in range(2):
            sp.dma_start(weights["L1_attn_w_out"][32 * n:32 * n + 32, i * SPAN:(i + 1) * SPAN]
                         .rearrange("d (j m) -> d j m", m=D),
                         dram["L1_attn_w_out"][i * SPAN + n * P:i * SPAN + (n + 1) * P, :]
                         .rearrange("(j d) m -> d j m", j=4)).then_inc(loaded, 16)
    sp.wait_ge(loaded, NEXT_LOADS * 16)


def setup(nc, dram, weights, consts, x_all, ctx_all, ctxT_all, xh_all):
    with ExitStack() as ctx:
        sem = ctx.enter_context(stage_semaphores(nc, "setup"))

        raw = {}
        for name, n in FIRST:
            raw[name] = ctx.enter_context(nc.sbuf_tensor(f"raw_{name}", [P, n * P], FP32))
        banks = [ctx.enter_context(nc.psum_tensor(f"turn{i}", [P, SPAN], FP32)) for i in range(8)]
        st = ctx.enter_context(nc.sbuf_tensor("st0", [P, NB, 6], FP32))
        mv = ctx.enter_context(nc.sbuf_tensor("mv0", [P, NB, 2], FP32))
        rstd = ctx.enter_context(nc.sbuf_tensor("rstd0", [P, 3, NB], FP32))
        qkv_loaded = [sem(f"qkv_loaded{i}") for i in range(3)]
        wout_loaded = sem("wout_loaded")
        x_loaded, ctx_loaded = sem("x_loaded"), sem("ctx_loaded")
        const_loaded, vectors_loaded = sem("const_loaded"), sem("vectors_loaded")
        turned = sem("turned")
        moved = [sem("moved_act"), sem("moved_dve")]
        stats, var_ready, bf_ready, xh_ready = sem("stats"), sem("var"), sem("bf"), sem("xh")
        pool_step, left = sem("pool_step"), sem("left")

        groups = []
        for first in range(0, NB, 4):
            groups.append(((ctx_loaded, 16), [ctx_all[:, (first + m) * P:(first + m + 1) * P] for m in range(4)],
                           ctxT_all[:, first * P:(first + 4) * P]))
        parts = []
        for name, n in FIRST:
            for first in range(0, n, 4):
                dst = weights[name][:, first * P:(first + 4) * P] if n == 8 or first < 16 else \
                    weights["wv_lead"][:, (first - 16) * P:(first - 12) * P]
                if n == 24 and first >= 16:
                    parts.append((len(groups), slice((first - 16) * P, (first - 12) * P)))
                ready = (qkv_loaded[first // 8], 16) if n == 24 else (wout_loaded, 64)
                groups.append((ready, [raw[name][:, (first + m) * P:(first + m + 1) * P] for m in range(4)],
                               dst))

        with nc.Block() as block:
            @block.sync
            def _(sp):
                sp.dma_start(x_all[:, :].rearrange("t (b d) -> t b d", b=NB),
                             dram["x"].rearrange("b t d -> t b d")).then_inc(x_loaded, 16)
                for i in range(3):
                    sp.dma_start(raw["L0_attn_w_qkv"][:, i * 8 * P:(i + 1) * 8 * P]
                                 .rearrange("p (n d) -> p n d", n=8),
                                 dram["L0_attn_w_qkv"][i * 8 * P:(i + 1) * 8 * P, :]
                                 .rearrange("(n p) d -> p n d", p=P)).then_inc(qkv_loaded[i], 16)
                src = dram["L0_attn_w_out"].rearrange("p (i n j d) -> p i j n d", n=4, j=2, d=64)
                dst = raw["L0_attn_w_out"][:, :].rearrange("p (i j n d) -> p i j n d", n=4, j=2, d=64)
                for i in range(2):
                    for j in range(2):
                        sp.dma_start(dst[:, i, j], src[:, i, j]).then_inc(wout_loaded, 16)

            @block.gpsimd
            def _(pool):
                pool.wait_ge(const_loaded, 16)
                pool.tensor_copy(consts["ident_bf"], consts["ident"]).then_inc(bf_ready, 1)
                pool.tensor_copy(consts["mask_bf"].rearrange("p (n k) -> p n k", n=4),
                                 consts["mask"].rearrange("p (o k) -> p o k", o=1)
                                 .broadcast_to([P, 4, P])).then_inc(bf_ready, 1)
                pool.wait_ge(var_ready, NB)
                link = linker(pool, pool_step)
                link(pool.tensor_scalar(rstd[:, 0, :], mv[:, :, 1], 1e-5, None, ALU.add))
                newton_rsqrt(pool, link, rstd[:, 1, :], rstd[:, 0, :], rstd[:, 2, :],
                             consts["neg_half"][:, 0:NB])

            @block.scalar
            def _(act):
                act.dma_start(consts["f32"], dram["const_f32"]).then_inc(const_loaded, 16)
                act.dma_start(ctx_all[:, :].rearrange("t (b d) -> t b d", b=NB),
                              dram["ctx_1024"].rearrange("b t d -> t b d")).then_inc(ctx_loaded, 16)
                for name in COLUMNS[0:2]:
                    act.dma_start(weights[name], dram[name].rearrange("(p o) -> p o", o=1))\
                       .then_inc(vectors_loaded, 16)
                act.dma_start(weights[ROWS[0]], dram[ROWS[0]].rearrange("(o n) -> o n", o=1)
                              .broadcast_to([P, P])).then_inc(vectors_loaded, 16)
                for n, (_, src, dst) in enumerate(groups):
                    if n % 2 == 0:
                        act.wait_ge(turned, n + 1)
                        act.activation(dst, banks[n % 8][:, :], ACT.Copy).then_inc(moved[0], 1)
                act.wait_ge(vectors_loaded, 48)

            @block.tensor
            def _(pe):
                pe.wait_ge(const_loaded, 16)
                for n, ((loaded, value), src, _) in enumerate(groups):
                    pe.wait_ge(loaded, value)
                    if n >= 8:
                        pe.wait_ge(moved[n % 2], n // 2 - 3)
                    for m, one in enumerate(src):
                        mm = pe.transpose(banks[n % 8][:, m * P:(m + 1) * P], one, consts["ident"])
                    mm.then_inc(turned, 1)

            @block.vector
            def _(dve):
                dve.wait_ge(x_loaded, 16)
                for b in range(NB):
                    dve.bn_stats(st[:, b, :], x_all[:, b * D:(b + 1) * D]).then_inc(stats, 1)
                for b in range(NB):
                    dve.wait_ge(stats, b + 1)
                    dve.bn_aggr(mv[:, b, :], st[:, b, :]).then_inc(var_ready, 1)
                dve.wait_ge(pool_step, 6)
                dve.wait_ge(var_ready, NB)
                for b in range(NB):
                    dve.tensor_scalar(xh_all[:, b * D:(b + 1) * D], x_all[:, b * D:(b + 1) * D],
                                      mv[:, b, 0:1], rstd[:, 1, b:b + 1], ALU.subtract, ALU.mult)\
                       .then_inc(xh_ready, 1)
                for n, (_, src, dst) in enumerate(groups):
                    if n % 2 == 1:
                        dve.wait_ge(turned, n + 1)
                        dve.tensor_copy(dst, banks[n % 8][:, :]).then_inc(moved[1], 1)
                for n, cols in parts:
                    dve.wait_ge(moved[n % 2], n // 2 + 1)
                    dve.tensor_tensor(weights["wv_left"][:, cols], banks[n % 8][:, :],
                                      weights["wv_lead"][:, cols].bitcast(FP32), op=ALU.subtract)\
                       .then_inc(left, 1)


CONST_COLS = {"ident": P, "before": P, "ones": P, "cos": P, "sin": P, "cos_q": P, "sin_q": P,
              "mask": P, "iota8": 8, "block_of": 4, "neg_half": NB}


def decoder(nc, dram, out, stages):
    with ExitStack() as ctx:
        def sb(name, shape, dt=FP32):
            return ctx.enter_context(nc.sbuf_tensor(name, shape, dt))

        x_all = sb("x_all", [P, NB * D])
        ctx_all = sb("ctx_all", [P, NB * D])
        ctxT_all = sb("ctxT_all", [P, NB * P])
        f32 = sb("const_f32_sb", [P, sum(CONST_COLS.values())])
        bf = sb("const_bf16_sb", [P, P + SPAN], BF16)
        consts = {"f32": f32[:, :], "ident_bf": bf[:, 0:P], "mask_bf": bf[:, P:]}
        at = 0
        for name, n in CONST_COLS.items():
            consts[name] = f32[:, at:at + n]
            at += n
        weights = {name: sb(f"w_{name}", [P, n * P]) for name, n in LATER}
        weights |= {name: sb(f"w_{name}", shape) for name, _, shape in PLAIN}
        weights["fc_lead"] = sb("fc_lead", [P, N_EXP * D_FF], FP32R)
        weights["fc_last_lead"] = sb("fc_last_lead", [P, N_EXP * P], FP32R)
        weights["proj_first"] = sb("proj_first", [P, N_EXP * D])
        weights["fc_last"] = sb("fc_last", [P, N_EXP * P])
        weights["proj_last"] = sb("proj_last", [P, N_EXP // 2 * D])
        cols = sb("columns", [P, len(COLUMNS) + 2])
        for n, name in enumerate(COLUMNS + ["L1_xattn_bq_turned", "L1_xattn_bk_turned"]):
            weights[name] = cols[:, n:n + 1]
        rows = sb("rows", [P, len(ROWS) * P])
        for n, name in enumerate(ROWS):
            weights[name] = rows[:, n * P:(n + 1) * P]
        out_done = ctx.enter_context(nc.semaphore("out_done"))
        later_loaded = ctx.enter_context(nc.semaphore("later_loaded"))
        kT_all, v_all = sb("kT_all", [P, NB * P]), sb("v_all", [P, NB * D])
        turned = sb("w_turned", [P, 2 * P])

        later = []
        with ExitStack() as part:
            xh_all = part.enter_context(nc.sbuf_tensor("xh_all", [P, NB * D], FP32))
            for name, n in FIRST:
                weights[name] = part.enter_context(nc.sbuf_tensor(f"w_{name}", [P, n * P], FP32))
            for name in ("wv_lead", "wv_left"):
                weights[name] = part.enter_context(nc.sbuf_tensor(f"L0_{name}", [P, 8 * P], FP32R))
            setup(nc, dram, weights, consts, x_all, ctx_all, ctxT_all, xh_all)
            if "A" in stages:
                attention_stage(nc, "causal", x_all, xh_all, consts,
                                {"wqkv": weights["L0_attn_w_qkv"], "wv_lead": weights["wv_lead"],
                                 "wv_left": weights["wv_left"],
                                 "wo": weights["L0_attn_w_out"],
                                 "bout": weights["L0_attn_b_out"],
                                 "gamma_col": weights["L0_attn_ln_gamma"],
                                 "beta_col": weights["L0_attn_ln_beta"]},
                                lambda sp: later.append(load_later(sp, dram, weights, later_loaded)))
        if "B" in stages:
            alignment_stage(nc, consts, x_all, ctx_all, ctxT_all, (later_loaded, later[0] * 16),
                            lambda part, sem: LaterWork(nc, part, sem, consts, weights, ctxT_all,
                                                        [turned[:, 0:P], turned[:, P:2 * P]], kT_all, v_all))
        weights["L1_attn_w_qkv"] = sb("w_L1_attn_w_qkv", [P, 3072])
        weights["L1_attn_w_out"] = sb("w_L1_attn_w_out", [P, 8 * D])
        wv_lead, wv_left = sb("L1_wv_lead", [P, 8 * P], FP32R), sb("L1_wv_left", [P, 8 * P], FP32R)
        if "C" in stages:
            experts_stage(nc, consts, weights, x_all,
                          lambda sp, loaded: load_second_attention(sp, dram, weights, loaded),
                          (weights["L1_attn_w_qkv"][:, 2 * 8 * P:], wv_lead[:, :], wv_left[:, :]))
        if "D" in stages:
            attention_stage(nc, "plain", x_all, x_all, consts,
                            {"wqkv": weights["L1_attn_w_qkv"], "wv_lead": wv_lead, "wv_left": wv_left,
                             "wo": weights["L1_attn_w_out"],
                             "bout": weights["L1_attn_b_out"], "gamma": weights["L1_attn_ln_gamma"],
                             "beta": weights["L1_attn_ln_beta"]})
        if "E" in stages:
            attention_stage(nc, "rope", x_all, x_all, consts | {"kT_all": kT_all, "v_all": v_all},
                            {"wq": weights["L1_xattn_Wq"][:, :], "wq_turned": turned[:, P:2 * P],
                             "bq": weights["L1_xattn_bq"], "bq_turned": weights["L1_xattn_bq_turned"],
                             "wo": weights["L1_xattn_Wo"][:, :], "bout": weights["L1_xattn_bo"]})
        if "F" in stages:
            with nc.sbuf_tensor("rnn_xT", [P, NB * P], FP32) as xT:
                turn_all(nc, "rnn", consts, x_all, xT)
                recurrent_stage(nc, consts, weights, x_all, xT)
        with nc.Block() as block:
            @block.sync
            def _(sp):
                sp.dma_start(out.rearrange("b t d -> t b d"),
                             x_all[:, :].rearrange("t (b d) -> t b d", b=NB)).then_inc(out_done, 16)
                sp.wait_ge(out_done, 16)


def constants():
    f = np.float32
    d = np.arange(P)
    inv = (1.0 / 10000.0 ** (np.arange(0, 8, 2, dtype=f) / f(8))).astype(f)
    angle = (np.arange(P, dtype=f)[None, :] * inv[d % 4][:, None]).astype(f)
    cos, sin = np.cos(angle.astype(np.float64)), np.sin(angle.astype(np.float64))
    sin = np.where((d % 8 < 4)[:, None], -sin, sin)
    parts = {"ident": np.eye(P), "before": np.triu(np.ones((P, P)), 1), "ones": np.ones((P, P)),
             "cos": cos, "sin": sin, "cos_q": cos * 8 ** -0.5, "sin_q": sin * 8 ** -0.5,
             "iota8": np.tile(np.arange(8), (P, 1)),
             "block_of": (d[:, None] // 8 % 4 == np.arange(4)[None, :]) * 1.0,
             "mask": np.where(d[None, :] > d[:, None], -BIG, 0.0),
             "neg_half": np.full((P, NB), -0.5)}
    f32 = np.concatenate([parts[n].astype(f) for n in CONST_COLS], axis=1)
    return f32


_OUTS = [((NB, P, D), "float32")]


def kernel(**inputs):
    import concourse.bacc as _bacc
    from concourse import mybir as _mybir
    from concourse.bass_utils import run_bass_kernel_spmd as _run

    nc = _bacc.Bacc("TRN2", target_bir_lowering=False, num_devices=1)
    arrays = {n: np.ascontiguousarray(a) for n, a in inputs.items()}
    arrays["const_f32"] = constants()
    for n in ("L1_xattn_bq", "L1_xattn_bk"):
        arrays[n + "_turned"] = np.ascontiguousarray(
            arrays[n].reshape(16, 2, 4)[:, ::-1, :].reshape(P))
    dram, given = {}, {}
    for n, a in arrays.items():
        given[f"in_{n}_dram"] = a
        dram[n] = nc.dram_tensor(f"in_{n}_dram", a.shape, _mybir.dt.from_np(a.dtype),
                                 kind="ExternalInput").ap()
    out = nc.dram_tensor("out_0_dram", _OUTS[0][0], _mybir.dt.float32, kind="ExternalOutput").ap()
    decoder(nc, dram, out, STAGES)
    r = _run(nc, [given], core_ids=[0])
    return r.results[0]["out_0_dram"]


STAGES = "ABCDEF"
```
